# Optimizing a Trainium2 kernel written in Bass

```python
import numpy as np
import jax
import jax.numpy as jnp

def _softmax(x, axis=-1):
    return jax.nn.softmax(x, axis=axis)

def _gelu(x):
    return jax.nn.gelu(x, approximate=True)

def _silu(x):
    return jax.nn.silu(x)

def _sigmoid(x):
    return jax.nn.sigmoid(x)

def _layernorm(x, axis=-1, eps=1e-05):
    m = jnp.mean(x, axis=axis, keepdims=True)
    v = jnp.var(x, axis=axis, keepdims=True)
    return (x - m) / jnp.sqrt(v + eps)

def _scatter_add(tgt, idx, src, axis=0):
    return tgt.at[idx].add(src)

def _segment_sum(src, seg, n):
    return jax.ops.segment_sum(src, seg, n)
kernel_name = 'mk_prb_d2_jaxref_r8_349605'

def setup_inputs(seed: int=0):
    np.random.seed(seed)
    _w = jnp.asarray

    def _L0_attn_setup():
        import jax, jax.numpy as jnp
        import numpy as np
        B, L, D = (4, 512, 128)
        PHAZOR_SCALE_START = 32.0
        PHAZOR_SCALE_END = 2048.0
        key = jax.random.key(seed)
        ks = jax.random.split(key, 7)
        x = jax.random.normal(ks[0], (B, L, D), dtype=jnp.float32)
        phazor_init_re = jax.random.normal(ks[1], (D,), dtype=jnp.float32)
        phazor_init_im = jax.random.normal(ks[2], (D,), dtype=jnp.float32)
        phazor_angle = jax.random.normal(ks[3], (D,), dtype=jnp.float32)
        ln_minus_ln_phazor_abs = jax.random.normal(ks[4], (D,), dtype=jnp.float32)
        last_conv_re = jax.random.normal(ks[5], (D,), dtype=jnp.float32)
        last_conv_im = jax.random.normal(ks[6], (D,), dtype=jnp.float32)
        ln_phazor_scale = jnp.exp(jnp.linspace(np.log(1.0 / PHAZOR_SCALE_START), np.log(1.0 / PHAZOR_SCALE_END), D)).astype(jnp.float32)
        return {'x': x, 'phazor_init_re': phazor_init_re, 'phazor_init_im': phazor_init_im, 'phazor_angle': phazor_angle, 'ln_minus_ln_phazor_abs': ln_minus_ln_phazor_abs, 'last_conv_re': last_conv_re, 'last_conv_im': last_conv_im, 'ln_phazor_scale': ln_phazor_scale}
    _L0_attn_in = _L0_attn_setup()

    def _L0_ffn_setup():
        import jax, jax.numpy as jnp
        import numpy as np
        DIM = 128

        def _reference_tuple_inner(x, W_r, W_k, W_v, mu_r, mu_k):
            B, T, C = x.shape
            x_prev = jnp.concatenate([jnp.zeros((B, 1, C), x.dtype), x[:, :-1, :]], axis=1)
            xr = mu_r * x + (1.0 - mu_r) * x_prev
            xk = mu_k * x + (1.0 - mu_k) * x_prev
            r = jax.nn.sigmoid(jnp.einsum('btc,dc->btd', xr, W_r))
            k = jnp.einsum('btc,dc->btd', xk, W_k)
            k_act = jnp.square(jax.nn.relu(k))
            out = r * jnp.einsum('btc,dc->btd', k_act, W_v)
            new_state = x[:, -1, :]
            return (out, new_state)
        key = jax.random.key(seed)
        ks = jax.random.split(key, 6)
        B, T, C = (8, 256, DIM)
        x = jax.random.normal(ks[0], (B, T, C), dtype=jnp.float32)
        s = 1.0 / np.sqrt(C)
        W_r = jax.random.uniform(ks[1], (C, C), jnp.float32, -s, s)
        W_k = jax.random.uniform(ks[2], (C, C), jnp.float32, -s, s)
        W_v = jax.random.uniform(ks[3], (C, C), jnp.float32, -s, s)
        mu_r = jax.random.uniform(ks[4], (C,), jnp.float32)
        mu_k = jax.random.uniform(ks[5], (C,), jnp.float32)
        return {'x': x, 'W_r': W_r, 'W_k': W_k, 'W_v': W_v, 'mu_r': mu_r, 'mu_k': mu_k}
    _L0_ffn_in = _L0_ffn_setup()

    def _L1_attn_setup():
        import jax, jax.numpy as jnp
        import numpy as np
        D_MODEL = 128
        D_STATE = 16
        D_CONV = 4
        EXPAND = 2
        D_INNER = EXPAND * D_MODEL
        DT_RANK = (D_MODEL + 15) // 16
        BATCH = 2
        SEQ = 256
        EPS = 1e-05

        def _mamba_params(key, scale=0.02):
            ks = jax.random.split(key, 8)
            n = lambda k, s: jax.random.normal(k, s, jnp.float32) * scale
            return {'Win': n(ks[0], (2 * D_INNER, D_MODEL)), 'convw': n(ks[1], (D_INNER, 1, D_CONV)), 'convb': n(ks[2], (D_INNER,)), 'Wx': n(ks[3], (DT_RANK + 2 * D_STATE, D_INNER)), 'Wdt': n(ks[4], (D_INNER, DT_RANK)), 'bdt': n(ks[5], (D_INNER,)), 'Alog': jnp.log(jnp.tile(jnp.arange(1, D_STATE + 1, dtype=jnp.float32), (D_INNER, 1))), 'D': jnp.ones((D_INNER,), jnp.float32), 'Wout': n(ks[6], (D_MODEL, D_INNER))}

        def _mamba(x, Win, convw, convb, Wx, Wdt, bdt, Alog, Dp, Wout):
            B, L, _ = x.shape
            xz = jnp.einsum('bld,ed->ble', x, Win)
            u, z = jnp.split(xz, 2, axis=-1)
            uc = jnp.transpose(u, (0, 2, 1))
            uc = jnp.pad(uc, ((0, 0), (0, 0), (D_CONV - 1, 0)))
            uc = jax.lax.conv_general_dilated(uc, convw, (1,), 'VALID', feature_group_count=D_INNER)
            uc = uc + convb[None, :, None]
            u = jax.nn.silu(jnp.transpose(uc, (0, 2, 1)))
            xdbl = jnp.einsum('bld,ed->ble', u, Wx)
            dtr, Bm, Cm = jnp.split(xdbl, [DT_RANK, DT_RANK + D_STATE], axis=-1)
            dt = jax.nn.softplus(jnp.einsum('blr,dr->bld', dtr, Wdt) + bdt)
            A = -jnp.exp(Alog)

            def step(h, ins):
                dt_t, u_t, B_t, C_t = ins
                h = jnp.exp(dt_t[..., None] * A) * h + (dt_t * u_t)[..., None] * B_t[:, None, :]
                y_t = jnp.einsum('bdn,bn->bd', h, C_t)
                return (h, y_t)
            h0 = jnp.zeros((B, D_INNER, D_STATE), jnp.float32)
            xs = (jnp.moveaxis(dt, 1, 0), jnp.moveaxis(u, 1, 0), jnp.moveaxis(Bm, 1, 0), jnp.moveaxis(Cm, 1, 0))
            _, ys = jax.lax.scan(step, h0, xs)
            y = jnp.moveaxis(ys, 0, 1) + u * Dp
            y = y * jax.nn.silu(z)
            return jnp.einsum('bld,ed->ble', y, Wout)
        key = jax.random.key(seed)
        kx, kf, kb = jax.random.split(key, 3)
        inp = {'x': jax.random.normal(kx, (BATCH, SEQ, D_MODEL), jnp.float32), 'norm_g': jnp.ones((D_MODEL,), jnp.float32), 'norm_b': jnp.zeros((D_MODEL,), jnp.float32)}
        for pfx, k in (('f', kf), ('b', kb)):
            for name, v in _mamba_params(k).items():
                inp[f'{pfx}_{name}'] = v
        return inp
    _L1_attn_in = _L1_attn_setup()

    def _L1_ffn_setup():
        import jax, jax.numpy as jnp
        import numpy as np
        B, S, H, NH, E, F = (4, 128, 128, 16, 8, 512)
        D = H // NH
        EPS = 1e-05

        def _layernorm(x, g, b):
            mu = jnp.mean(x, axis=-1, keepdims=True)
            var = jnp.var(x, axis=-1, keepdims=True)
            return (x - mu) * jax.lax.rsqrt(var + EPS) * g + b
        key = jax.random.key(seed)
        ks = jax.random.split(key, 16)
        s = 0.02
        return {'x': jax.random.normal(ks[0], (B, S, H), jnp.float32), 'ln1_g': jnp.ones((H,), jnp.float32), 'ln1_b': jnp.zeros((H,), jnp.float32), 'ln2_g': jnp.ones((H,), jnp.float32), 'ln2_b': jnp.zeros((H,), jnp.float32), 'wq': jax.random.normal(ks[1], (H, H), jnp.float32) * s, 'bq': jnp.zeros((H,), jnp.float32), 'wk': jax.random.normal(ks[2], (H, H), jnp.float32) * s, 'bk': jnp.zeros((H,), jnp.float32), 'wv': jax.random.normal(ks[3], (H, H), jnp.float32) * s, 'bv': jnp.zeros((H,), jnp.float32), 'wo': jax.random.normal(ks[4], (H, H), jnp.float32) * s, 'bo': jnp.zeros((H,), jnp.float32), 'gate_w': jax.random.normal(ks[5], (H, E), jnp.float32) * s, 'gate_b': jnp.zeros((E,), jnp.float32), 'w1': jax.random.normal(ks[6], (E, H, F), jnp.float32) * s, 'b1': jnp.zeros((E, F), jnp.float32), 'w2': jax.random.normal(ks[7], (E, F, H), jnp.float32) * s, 'b2': jnp.zeros((E, H), jnp.float32)}
    _L1_ffn_in = _L1_ffn_setup()
    _d = {'L0_attn_x': _L0_attn_in['x'], 'L0_attn_phazor_init_re': _L0_attn_in['phazor_init_re'], 'L0_attn_phazor_init_im': _L0_attn_in['phazor_init_im'], 'L0_attn_phazor_angle': _L0_attn_in['phazor_angle'], 'L0_attn_ln_minus_ln_phazor_abs': _L0_attn_in['ln_minus_ln_phazor_abs'], 'L0_attn_last_conv_re': _L0_attn_in['last_conv_re'], 'L0_attn_last_conv_im': _L0_attn_in['last_conv_im'], 'L0_attn_ln_phazor_scale': _L0_attn_in['ln_phazor_scale'], 'L0_ffn_W_r': _L0_ffn_in['W_r'], 'L0_ffn_W_k': _L0_ffn_in['W_k'], 'L0_ffn_W_v': _L0_ffn_in['W_v'], 'L0_ffn_mu_r': _L0_ffn_in['mu_r'], 'L0_ffn_mu_k': _L0_ffn_in['mu_k'], 'L1_attn_norm_g': _L1_attn_in['norm_g'], 'L1_attn_norm_b': _L1_attn_in['norm_b'], 'L1_attn_f_Win': _L1_attn_in['f_Win'], 'L1_attn_f_convw': _L1_attn_in['f_convw'], 'L1_attn_f_convb': _L1_attn_in['f_convb'], 'L1_attn_f_Wx': _L1_attn_in['f_Wx'], 'L1_attn_f_Wdt': _L1_attn_in['f_Wdt'], 'L1_attn_f_bdt': _L1_attn_in['f_bdt'], 'L1_attn_f_Alog': _L1_attn_in['f_Alog'], 'L1_attn_f_D': _L1_attn_in['f_D'], 'L1_attn_f_Wout': _L1_attn_in['f_Wout'], 'L1_attn_b_Win': _L1_attn_in['b_Win'], 'L1_attn_b_convw': _L1_attn_in['b_convw'], 'L1_attn_b_convb': _L1_attn_in['b_convb'], 'L1_attn_b_Wx': _L1_attn_in['b_Wx'], 'L1_attn_b_Wdt': _L1_attn_in['b_Wdt'], 'L1_attn_b_bdt': _L1_attn_in['b_bdt'], 'L1_attn_b_Alog': _L1_attn_in['b_Alog'], 'L1_attn_b_D': _L1_attn_in['b_D'], 'L1_attn_b_Wout': _L1_attn_in['b_Wout'], 'L1_ffn_ln1_g': _L1_ffn_in['ln1_g'], 'L1_ffn_ln1_b': _L1_ffn_in['ln1_b'], 'L1_ffn_ln2_g': _L1_ffn_in['ln2_g'], 'L1_ffn_ln2_b': _L1_ffn_in['ln2_b'], 'L1_ffn_wq': _L1_ffn_in['wq'], 'L1_ffn_bq': _L1_ffn_in['bq'], 'L1_ffn_wk': _L1_ffn_in['wk'], 'L1_ffn_bk': _L1_ffn_in['bk'], 'L1_ffn_wv': _L1_ffn_in['wv'], 'L1_ffn_bv': _L1_ffn_in['bv'], 'L1_ffn_wo': _L1_ffn_in['wo'], 'L1_ffn_bo': _L1_ffn_in['bo'], 'L1_ffn_gate_w': _L1_ffn_in['gate_w'], 'L1_ffn_gate_b': _L1_ffn_in['gate_b'], 'L1_ffn_w1': _L1_ffn_in['w1'], 'L1_ffn_b1': _L1_ffn_in['b1'], 'L1_ffn_w2': _L1_ffn_in['w2'], 'L1_ffn_b2': _L1_ffn_in['b2']}
    _x0 = _d['L0_attn_x']
    _d['L0_attn_x'] = jax.random.normal(jax.random.fold_in(jax.random.key(seed), 1), (1, 2048, 128), dtype=_x0.dtype)
    del _x0
    return _d

def reference(L0_attn_x, L0_attn_phazor_init_re, L0_attn_phazor_init_im, L0_attn_phazor_angle, L0_attn_ln_minus_ln_phazor_abs, L0_attn_last_conv_re, L0_attn_last_conv_im, L0_attn_ln_phazor_scale, L0_ffn_W_r, L0_ffn_W_k, L0_ffn_W_v, L0_ffn_mu_r, L0_ffn_mu_k, L1_attn_norm_g, L1_attn_norm_b, L1_attn_f_Win, L1_attn_f_convw, L1_attn_f_convb, L1_attn_f_Wx, L1_attn_f_Wdt, L1_attn_f_bdt, L1_attn_f_Alog, L1_attn_f_D, L1_attn_f_Wout, L1_attn_b_Win, L1_attn_b_convw, L1_attn_b_convb, L1_attn_b_Wx, L1_attn_b_Wdt, L1_attn_b_bdt, L1_attn_b_Alog, L1_attn_b_D, L1_attn_b_Wout, L1_ffn_ln1_g, L1_ffn_ln1_b, L1_ffn_ln2_g, L1_ffn_ln2_b, L1_ffn_wq, L1_ffn_bq, L1_ffn_wk, L1_ffn_bk, L1_ffn_wv, L1_ffn_bv, L1_ffn_wo, L1_ffn_bo, L1_ffn_gate_w, L1_ffn_gate_b, L1_ffn_w1, L1_ffn_b1, L1_ffn_w2, L1_ffn_b2):

    def _L0_attn_ref(x, phazor_init_re, phazor_init_im, phazor_angle, ln_minus_ln_phazor_abs, last_conv_re, last_conv_im, ln_phazor_scale):
        import jax, jax.numpy as jnp
        import numpy as np
        B, L, D = (4, 512, 128)
        PHAZOR_SCALE_START = 32.0
        PHAZOR_SCALE_END = 2048.0
        b, length, d = x.shape
        dtype = x.dtype
        xc = x.astype(jnp.complex64)
        decay = jnp.exp(ln_minus_ln_phazor_abs)
        phazor = jnp.exp((phazor_angle * 1j - decay) * ln_phazor_scale)
        t = jnp.arange(length, dtype=jnp.float32)[:, None]
        phazor_progression = phazor[None, :] ** t
        phazor_init = phazor_init_re + 1j * phazor_init_im
        filt = phazor_progression * phazor_init[None, :]
        filter_fft = jnp.fft.fft(filt, n=2 * length, axis=0)
        x_fft = jnp.fft.fft(xc, n=2 * length, axis=1)
        conv_filter_x = jnp.fft.ifft(filter_fft[None] * x_fft, axis=1)[:, :length]
        last_conv = (last_conv_re + 1j * last_conv_im)[None, None, :]
        conv_with_past = conv_filter_x + last_conv * phazor_progression[None] * phazor[None, None, :]
        gate = 1.0 - jnp.exp(-decay * ln_phazor_scale)
        y = conv_with_past * gate
        return y.real.astype(dtype)

    def _L0_ffn_ref(x, W_r, W_k, W_v, mu_r, mu_k):
        import jax, jax.numpy as jnp
        import numpy as np
        DIM = 128

        def _reference_tuple_inner(x, W_r, W_k, W_v, mu_r, mu_k):
            B, T, C = x.shape
            x_prev = jnp.concatenate([jnp.zeros((B, 1, C), x.dtype), x[:, :-1, :]], axis=1)
            xr = mu_r * x + (1.0 - mu_r) * x_prev
            xk = mu_k * x + (1.0 - mu_k) * x_prev
            r = jax.nn.sigmoid(jnp.einsum('btc,dc->btd', xr, W_r))
            k = jnp.einsum('btc,dc->btd', xk, W_k)
            k_act = jnp.square(jax.nn.relu(k))
            out = r * jnp.einsum('btc,dc->btd', k_act, W_v)
            new_state = x[:, -1, :]
            return (out, new_state)
        return _reference_tuple_inner(x, W_r, W_k, W_v, mu_r, mu_k)[0]

    def _L1_attn_ref(x, norm_g, norm_b, f_Win, f_convw, f_convb, f_Wx, f_Wdt, f_bdt, f_Alog, f_D, f_Wout, b_Win, b_convw, b_convb, b_Wx, b_Wdt, b_bdt, b_Alog, b_D, b_Wout):
        import jax, jax.numpy as jnp
        import numpy as np
        D_MODEL = 128
        D_STATE = 16
        D_CONV = 4
        EXPAND = 2
        D_INNER = EXPAND * D_MODEL
        DT_RANK = (D_MODEL + 15) // 16
        BATCH = 2
        SEQ = 256
        EPS = 1e-05

        def _mamba_params(key, scale=0.02):
            ks = jax.random.split(key, 8)
            n = lambda k, s: jax.random.normal(k, s, jnp.float32) * scale
            return {'Win': n(ks[0], (2 * D_INNER, D_MODEL)), 'convw': n(ks[1], (D_INNER, 1, D_CONV)), 'convb': n(ks[2], (D_INNER,)), 'Wx': n(ks[3], (DT_RANK + 2 * D_STATE, D_INNER)), 'Wdt': n(ks[4], (D_INNER, DT_RANK)), 'bdt': n(ks[5], (D_INNER,)), 'Alog': jnp.log(jnp.tile(jnp.arange(1, D_STATE + 1, dtype=jnp.float32), (D_INNER, 1))), 'D': jnp.ones((D_INNER,), jnp.float32), 'Wout': n(ks[6], (D_MODEL, D_INNER))}

        def _mamba(x, Win, convw, convb, Wx, Wdt, bdt, Alog, Dp, Wout):
            B, L, _ = x.shape
            xz = jnp.einsum('bld,ed->ble', x, Win)
            u, z = jnp.split(xz, 2, axis=-1)
            uc = jnp.transpose(u, (0, 2, 1))
            uc = jnp.pad(uc, ((0, 0), (0, 0), (D_CONV - 1, 0)))
            uc = jax.lax.conv_general_dilated(uc, convw, (1,), 'VALID', feature_group_count=D_INNER)
            uc = uc + convb[None, :, None]
            u = jax.nn.silu(jnp.transpose(uc, (0, 2, 1)))
            xdbl = jnp.einsum('bld,ed->ble', u, Wx)
            dtr, Bm, Cm = jnp.split(xdbl, [DT_RANK, DT_RANK + D_STATE], axis=-1)
            dt = jax.nn.softplus(jnp.einsum('blr,dr->bld', dtr, Wdt) + bdt)
            A = -jnp.exp(Alog)

            def step(h, ins):
                dt_t, u_t, B_t, C_t = ins
                h = jnp.exp(dt_t[..., None] * A) * h + (dt_t * u_t)[..., None] * B_t[:, None, :]
                y_t = jnp.einsum('bdn,bn->bd', h, C_t)
                return (h, y_t)
            h0 = jnp.zeros((B, D_INNER, D_STATE), jnp.float32)
            xs = (jnp.moveaxis(dt, 1, 0), jnp.moveaxis(u, 1, 0), jnp.moveaxis(Bm, 1, 0), jnp.moveaxis(Cm, 1, 0))
            _, ys = jax.lax.scan(step, h0, xs)
            y = jnp.moveaxis(ys, 0, 1) + u * Dp
            y = y * jax.nn.silu(z)
            return jnp.einsum('bld,ed->ble', y, Wout)
        mu = jnp.mean(x, axis=-1, keepdims=True)
        var = jnp.var(x, axis=-1, keepdims=True)
        xn = (x - mu) * jax.lax.rsqrt(var + EPS) * norm_g + norm_b
        y_fwd = _mamba(xn, f_Win, f_convw, f_convb, f_Wx, f_Wdt, f_bdt, f_Alog, f_D, f_Wout)
        y_bwd = _mamba(jnp.flip(xn, axis=1), b_Win, b_convw, b_convb, b_Wx, b_Wdt, b_bdt, b_Alog, b_D, b_Wout)
        y_bwd = jnp.flip(y_bwd, axis=1)
        return x + y_fwd + y_bwd

    def _L1_ffn_ref(x, ln1_g, ln1_b, ln2_g, ln2_b, wq, bq, wk, bk, wv, bv, wo, bo, gate_w, gate_b, w1, b1, w2, b2):
        import jax, jax.numpy as jnp
        import numpy as np
        B, S, H, NH, E, F = (4, 128, 128, 16, 8, 512)
        D = H // NH
        EPS = 1e-05

        def _layernorm(x, g, b):
            mu = jnp.mean(x, axis=-1, keepdims=True)
            var = jnp.var(x, axis=-1, keepdims=True)
            return (x - mu) * jax.lax.rsqrt(var + EPS) * g + b
        b, s, h = x.shape
        hn = _layernorm(x, ln1_g, ln1_b)
        q = (hn @ wq + bq).reshape(b, s, NH, D).transpose(0, 2, 1, 3)
        k = (hn @ wk + bk).reshape(b, s, NH, D).transpose(0, 2, 1, 3)
        v = (hn @ wv + bv).reshape(b, s, NH, D).transpose(0, 2, 1, 3)
        scores = jnp.einsum('bhqd,bhkd->bhqk', q, k) / jnp.sqrt(jnp.float32(D))
        attn = jax.nn.softmax(scores, axis=-1)
        o = jnp.einsum('bhqk,bhkd->bhqd', attn, v)
        o = o.transpose(0, 2, 1, 3).reshape(b, s, h)
        x = x + (o @ wo + bo)
        hn2 = _layernorm(x, ln2_g, ln2_b).reshape(-1, h)
        logits = hn2 @ gate_w + gate_b
        idx = jnp.argmax(logits, axis=-1)
        mid = jax.nn.relu(jnp.einsum('th,ehf->etf', hn2, w1) + b1[:, None, :])
        y = jnp.einsum('etf,efh->eth', mid, w2) + b2[:, None, :]
        moe = y[idx, jnp.arange(hn2.shape[0])]
        return x + moe.reshape(b, s, h)
    x = L0_attn_x
    xn = _layernorm(x, axis=-1)
    x = x + _L0_attn_ref(xn, L0_attn_phazor_init_re, L0_attn_phazor_init_im, L0_attn_phazor_angle, L0_attn_ln_minus_ln_phazor_abs, L0_attn_last_conv_re, L0_attn_last_conv_im, L0_attn_ln_phazor_scale) + _L0_ffn_ref(xn, L0_ffn_W_r, L0_ffn_W_k, L0_ffn_W_v, L0_ffn_mu_r, L0_ffn_mu_k)
    xn = _layernorm(x, axis=-1)
    x = x + _L1_attn_ref(xn, L1_attn_norm_g, L1_attn_norm_b, L1_attn_f_Win, L1_attn_f_convw, L1_attn_f_convb, L1_attn_f_Wx, L1_attn_f_Wdt, L1_attn_f_bdt, L1_attn_f_Alog, L1_attn_f_D, L1_attn_f_Wout, L1_attn_b_Win, L1_attn_b_convw, L1_attn_b_convb, L1_attn_b_Wx, L1_attn_b_Wdt, L1_attn_b_bdt, L1_attn_b_Alog, L1_attn_b_D, L1_attn_b_Wout) + _L1_ffn_ref(xn, L1_ffn_ln1_g, L1_ffn_ln1_b, L1_ffn_ln2_g, L1_ffn_ln2_b, L1_ffn_wq, L1_ffn_bq, L1_ffn_wk, L1_ffn_bk, L1_ffn_wv, L1_ffn_bv, L1_ffn_wo, L1_ffn_bo, L1_ffn_gate_w, L1_ffn_gate_b, L1_ffn_w1, L1_ffn_b1, L1_ffn_w2, L1_ffn_b2)
    return x

_drawn_inputs = setup_inputs


def setup_inputs(seed=0):
    import zlib

    import numpy as np

    out = dict(_drawn_inputs(seed))
    spreads = {'L1_attn_norm_g': (1.0, 0.6),
     'L1_attn_norm_b': (0.0, 0.8),
     'L1_attn_f_D': (1.0, 0.6),
     'L1_attn_b_D': (1.0, 0.6),
     'L1_ffn_ln1_g': (1.0, 0.6),
     'L1_ffn_ln1_b': (0.0, 0.8),
     'L1_ffn_ln2_g': (1.0, 0.6),
     'L1_ffn_ln2_b': (0.0, 2.0),
     'L1_ffn_bq': (0.0, 0.8),
     'L1_ffn_bk': (0.0, 2.0),
     'L1_ffn_bv': (0.0, 0.647),
     'L1_ffn_bo': (0.0, 0.8),
     'L1_ffn_gate_b': (0.0, 1.566),
     'L1_ffn_b1': (0.0, 2.0),
     'L1_ffn_b2': (0.0, 0.8)}
    factors = {'L0_attn_last_conv_re': 27.62,
     'L0_attn_last_conv_im': 51.717,
     'L0_ffn_W_r': 2.938,
     'L0_ffn_mu_r': 5.554,
     'L1_attn_f_Win': 8.0,
     'L1_attn_f_convw': 8.0,
     'L1_attn_f_convb': 8.0,
     'L1_attn_f_Wx': 8.0,
     'L1_attn_f_bdt': 8.0,
     'L1_attn_f_Alog': 8.0,
     'L1_attn_f_Wout': 8.0,
     'L1_attn_b_Win': 8.0,
     'L1_attn_b_convw': 8.0,
     'L1_attn_b_convb': 8.0,
     'L1_attn_b_Wx': 8.0,
     'L1_attn_b_bdt': 8.0,
     'L1_attn_b_Alog': 8.0,
     'L1_attn_b_Wout': 8.0,
     'L1_ffn_wq': 8.0,
     'L1_ffn_wk': 8.0,
     'L1_ffn_wv': 8.0,
     'L1_ffn_wo': 5.663,
     'L1_ffn_w1': 14.623,
     'L1_ffn_gate_w': 3.641,
     'L1_ffn_w2': 3.594}
    for name, (base, spread) in spreads.items():
        noise = np.random.default_rng([zlib.crc32(name.encode()), seed]).standard_normal(out[name].shape)
        drawn = base * np.exp(spread * noise) if base else spread * noise
        out[name] = jnp.asarray(drawn.astype(out[name].dtype))
    for name, factor in factors.items():
        out[name] = (out[name] * factor).astype(out[name].dtype)
    return out
```

```python
from contextlib import ExitStack

import numpy as np

import concourse.bass as bass
from concourse import mybir

F32 = mybir.dt.float32
BF16 = mybir.dt.bfloat16
I32 = mybir.dt.int32
ALU = mybir.AluOpType
ACT = mybir.ActivationFunctionType
AX = mybir.AxisListType

P = 128
T = 2048
NT = T // P
CH = 512
NCH = T // CH
TPC = CH // P
EPS = 1e-5
TWO_PI = 2 * np.pi
SIN_SCALE = 6.283185
ROUND = 12582912.0

NH, HD = 16, 8
NE, NF = 8, 512
NFB = NF // P
DI, NS, KC, DR = 256, 16, 4, 8
NB = DI // P

VECS = ["init_re", "init_im", "angle", "lnml", "lc_re", "lc_im", "ln_scale", "mu_r", "mu_k",
        "norm_g", "norm_b", "ln1_g", "ln1_b", "ln2_g", "ln2_b", "bq", "bk"]
for _d in "fb":
    VECS += [f"{_d}_{n}{b}" for n in ("convb", "bdt", "D") for b in range(NB)]
    VECS += [f"{_d}_convw{b}{k}" for b in range(NB) for k in range(KC)]
    VECS += [f"{_d}_Alog{b}_{s}" for b in range(NB) for s in range(NS)]
VCOL = {n: i for i, n in enumerate(VECS)}
NV = len(VECS)


class Shared:

    def enter_sem(self, nc, name):
        handle = nc.alloc_semaphore(name=name)
        self.sems.append(handle)
        return handle

    def end_stage(self, nc):
        nc.clear_and_free_semaphores(self.sems)
        nc.all_engine_barrier()
        self.sems = []


def natural(dram):
    return dram.rearrange("o (i p) d -> p (o i) d", p=P)


def layer0_stage(nc, S, dr):
    with ExitStack() as ctx:
        def sb(name, shape, dt=F32):
            return ctx.enter_context(nc.sbuf_tensor(name, shape, dt))

        def sem(name):
            return S.enter_sem(nc, name)

        X = sb("l0_x", [P, NT, P])
        XN = sb("l0_xn", [P, NT, P])
        st6 = sb("l0_st6", [P, NT, 6])
        mv = sb("l0_mv", [P, NT, 2])
        rstd = sb("l0_rstd", [P, NT])
        lnv = sb("l0_lnv", [P, NT])
        rstd2 = sb("l0_rstd2", [P, NT])
        w2v = sb("l0_w2v", [P, NT])
        xpad = sb("l0_xpad", [P, T + 1])
        xT = xpad[:, 1:T + 1]
        x_prev = xpad[:, 0:T]
        ti = sb("l0_ti", [P, T], I32)
        turns = sb("l0_turns", [P, T])
        whole = sb("l0_whole", [P, T])
        sinT = sb("l0_sin", [P, T])
        cosT = sb("l0_cos", [P, T])
        p_re = sb("l0_pre", [P, T])
        p_im = sb("l0_pim", [P, T])
        s_mix = sb("l0_mix", [P, T])
        dx = sb("l0_dx", [P, T])
        xr = sb("l0_xr", [P, T])
        xk = sb("l0_xk", [P, T])
        sig = sb("l0_sig", [P, T])
        kact = sb("l0_kact", [P, T])
        W = sb("l0_w", [P, 3, P])
        sc = sb("l0_sc", [P, 16])
        (decay, dec_s, r_abs, gate, freq, a_re, a_im, na_im, l_re, l_im, tmp1, tmp2, in_re, in_im, tmp3,
         _) = [sc[:, i:i + 1] for i in range(16)]
        ident_w = S.ident

        banks = S.banks

        x_in = [sem(f"l0_x_in{q}") for q in range(4)]
        vec_in, w_in = sem("l0_vec_in"), sem("l0_w_in")
        pool_c, dve_c, act_c = sem("l0_pool_chain"), sem("l0_dve_chain"), sem("l0_act_chain")
        ident_ready = sem("l0_ident_ready")
        tok_ready = sem("l0_tok_ready")
        decay_ready, decs_ready, rabs_ready = sem("l0_decay"), sem("l0_decs"), sem("l0_rabs")
        turn_ready, trig_ready, turn_free = sem("l0_turn"), sem("l0_trig"), sem("l0_turn_free")
        var_ready, rstd_ready, xn_ready = sem("l0_var"), sem("l0_rstd_r"), sem("l0_xn_r")
        xT_psum, xT_ready = sem("l0_xT_psum"), sem("l0_xT_r")
        dx_ready, mixin_ready = sem("l0_dx_r"), sem("l0_mixin")
        proj_done, act_done, sq_done, val_done = sem("l0_proj"), sem("l0_actd"), sem("l0_sq"), sem("l0_val")
        mix_ready, back_done = sem("l0_mix_r"), sem("l0_back")
        var1_ready, rstd1_ready, w2_ready, rstd2_ready = sem("l0_v1"), sem("l0_r1"), sem("l0_w2"), sem("l0_r2")
        xh_ready, xh_psum, val_free = sem("l0_xh"), sem("l0_xhp"), sem("l0_vfree")
        block = ctx.enter_context(nc.Block())

        def V(name):
            return S.vec[:, VCOL[name]:VCOL[name] + 1]

        @block.sync
        def _(sp):
            sp.dma_start(S.vec[:, :], dr["vecs"]).then_inc(vec_in, 16)
            for q in range(4):
                sp.dma_start(X[:, 4 * q:4 * q + 4, :], natural(dr["x"])[:, 4 * q:4 * q + 4, :]).then_inc(x_in[q], 16)
            sp.dma_start(W[:, :, :], dr["w_mix"].rearrange("m c d -> c m d")).then_inc(w_in, 16)
            sp.wait_ge(w_in, 16)

        @block.gpsimd
        def _(pool):
            pool.iota(ti[:, :], pattern=[[1, T]], base=0, channel_multiplier=0).then_inc(tok_ready, 1)
            pool.memset(S.ident[:, :], 0.0).then_inc(pool_c, 1)
            pool.memset(S.flip[:, :], 0.0).then_inc(pool_c, 1)
            pool.memset(xpad[:, 0:1], 0.0).then_inc(pool_c, 1)
            pool.wait_ge(pool_c, 3)
            pool.affine_select(out=S.ident[:, :], in_=S.ident[:, :], compare_op=ALU.not_equal, fill=1.0,
                               base=0, pattern=[[-1, P]], channel_multiplier=1).then_inc(ident_ready, 1)
            pool.affine_select(out=S.flip[:, :], in_=S.flip[:, :], compare_op=ALU.not_equal, fill=1.0,
                               base=-(P - 1), pattern=[[1, P]], channel_multiplier=1).then_inc(ident_ready, 1)
            pool.wait_ge(xT_ready, NCH)
            pool.tensor_tensor(dx[:, :], xT, x_prev, ALU.subtract).then_inc(dx_ready, 1)
            for c in range(NCH):
                pool.wait_ge(act_done, 2 * c + 2)
                pool.tensor_tensor(kact[:, c * CH:(c + 1) * CH], kact[:, c * CH:(c + 1) * CH],
                                   kact[:, c * CH:(c + 1) * CH], ALU.mult).then_inc(sq_done, 1)

        @block.scalar
        def _(act):
            act.wait_ge(vec_in, 16)
            act.activation(decay, V("lnml"), ACT.Exp).then_inc(decay_ready, 1)
            act.wait_ge(decs_ready, 1)
            act.activation(r_abs, dec_s, ACT.Exp, scale=-1.0).then_inc(rabs_ready, 1)
            act.wait_ge(var_ready, 1)
            act.activation(lnv[:, :], w2v[:, :], ACT.Ln).then_inc(act_c, 1)
            act.wait_ge(act_c, 1)
            act.activation(rstd[:, :], lnv[:, :], ACT.Exp, scale=-0.5).then_inc(rstd_ready, 1)
            for c in range(NCH):
                act.wait_ge(xT_psum, c + 1)
                act.activation(xpad[:, 1 + c * CH:1 + (c + 1) * CH], banks[c][:, :], ACT.Copy).then_inc(xT_ready, 1)
            act.wait_ge(turn_ready, 1)
            act.activation(sinT[:, :], turns[:, :], ACT.Sin, scale=SIN_SCALE).then_inc(trig_ready, 1)
            act.wait_ge(turn_ready, 2)
            act.activation(cosT[:, :], whole[:, :], ACT.Sin, scale=SIN_SCALE).then_inc(trig_ready, 1)
            for c in range(NCH):
                act.wait_ge(proj_done, 2 * c + 1)
                act.activation(sig[:, c * CH:(c + 1) * CH], banks[2 * (c % 2)][:, :], ACT.Sigmoid).then_inc(act_done, 1)
                act.wait_ge(proj_done, 2 * c + 2)
                act.activation(kact[:, c * CH:(c + 1) * CH], banks[2 * (c % 2) + 1][:, :], ACT.Relu).then_inc(act_done, 1)
            act.wait_ge(var1_ready, 1)
            act.activation(lnv[:, :], w2v[:, :], ACT.Ln).then_inc(act_c, 1)
            act.wait_ge(act_c, 2)
            act.activation(rstd[:, :], lnv[:, :], ACT.Exp, scale=-0.5).then_inc(rstd1_ready, 1)
            act.wait_ge(w2_ready, 1)
            act.activation(lnv[:, :], w2v[:, :], ACT.Ln).then_inc(act_c, 1)
            act.wait_ge(act_c, 3)
            act.activation(rstd2[:, :], lnv[:, :], ACT.Exp, scale=-0.5).then_inc(rstd2_ready, 1)
            for c in range(NCH):
                act.wait_ge(xh_psum, 2 * c + 1)
                act.activation(S.xh[:, 0, c * CH:(c + 1) * CH], banks[c][:, :], ACT.Copy).then_inc(act_c, 1)
                act.wait_ge(xh_psum, 2 * c + 2)
                act.activation(S.xh[:, 1, T - (c + 1) * CH:T - c * CH], banks[4 + c][:, :], ACT.Copy).then_inc(act_c, 1)

        @block.vector
        def _(dve):
            count = [0]

            def link(ins):
                count[0] += 1
                ins.then_inc(dve_c, 1)
                dve.wait_ge(dve_c, count[0])

            dve.wait_ge(vec_in, 16)
            dve.wait_ge(decay_ready, 1)
            dve.tensor_tensor(dec_s, decay, V("ln_scale"), ALU.mult).then_inc(decs_ready, 1)
            link(dve.tensor_scalar(freq, V("angle"), V("ln_scale"), 1.0 / TWO_PI, ALU.mult, ALU.mult))
            for q in range(4):
                dve.wait_ge(x_in[q], 16)
                for i in range(4 * q, 4 * q + 4):
                    last = dve.bn_stats(st6[:, i, :], X[:, i, :])
            link(last)
            for i in range(NT):
                last = dve.bn_aggr(mv[:, i, :], st6[:, i, :])
            link(last)
            dve.tensor_scalar(w2v[:, :], mv[:, :, 1], EPS, None, ALU.add).then_inc(var_ready, 1)
            dve.wait_ge(rstd_ready, 1)
            for i in range(NT):
                dve.tensor_scalar(XN[:, i, :], X[:, i, :], mv[:, i, 0:1], rstd[:, i:i + 1],
                                  ALU.subtract, ALU.mult).then_inc(xn_ready, 1)
            dve.wait_ge(tok_ready, 1)
            link(dve.tensor_copy(sinT[:, :], ti[:, :]))
            link(dve.tensor_scalar(turns[:, :], sinT[:, :], freq, None, ALU.mult))
            link(dve.tensor_scalar(whole[:, :], turns[:, :], ROUND, -ROUND, ALU.add, ALU.add))
            link(dve.tensor_tensor(turns[:, :], turns[:, :], whole[:, :], ALU.subtract))
            link(dve.tensor_scalar(p_re[:, :], turns[:, :], 0.25, None, ALU.add))
            link(dve.tensor_scalar(p_im[:, :], p_re[:, :], ROUND, -ROUND, ALU.add, ALU.add))
            dve.sem_inc(turn_ready, 1)
            link(dve.tensor_tensor(whole[:, :], p_re[:, :], p_im[:, :], ALU.subtract))
            dve.sem_inc(turn_ready, 1)
            dve.wait_ge(rabs_ready, 1)
            link(dve.tensor_scalar(gate, r_abs, -1.0, 1.0, ALU.mult, ALU.add))
            dve.tensor_tensor(a_re, V("init_re"), gate, ALU.mult)
            dve.tensor_tensor(l_re, V("lc_re"), gate, ALU.mult)
            dve.tensor_tensor(l_im, V("lc_im"), gate, ALU.mult)
            link(dve.tensor_tensor(a_im, V("init_im"), gate, ALU.mult))
            link(dve.tensor_scalar(na_im, a_im, -1.0, None, ALU.mult))
            dve.wait_ge(trig_ready, 2)
            dve.tensor_tensor(tmp1, l_re, cosT[:, 1:2], ALU.mult)
            dve.tensor_tensor(tmp2, l_im, sinT[:, 1:2], ALU.mult)
            link(dve.tensor_tensor(tmp3, l_re, sinT[:, 1:2], ALU.mult))
            dve.tensor_tensor(in_re, tmp1, tmp2, ALU.subtract)
            link(dve.scalar_tensor_tensor(out=in_im, in0=l_im, scalar=cosT[:, 1:2], in1=tmp3,
                                          op0=ALU.mult, op1=ALU.add))
            dve.tensor_scalar(p_re[:, :], cosT[:, :], a_re, None, ALU.mult)
            link(dve.tensor_scalar(p_im[:, :], cosT[:, :], a_im, None, ALU.mult))
            dve.scalar_tensor_tensor(out=p_re[:, :], in0=sinT[:, :], scalar=a_im, in1=p_re[:, :],
                                     op0=ALU.mult, op1=ALU.add)
            dve.wait_ge(xT_ready, NCH)
            link(dve.tensor_scalar(tmp1, a_re, -1.0, None, ALU.mult))
            link(dve.scalar_tensor_tensor(out=p_im[:, :], in0=sinT[:, :], scalar=tmp1, in1=p_im[:, :],
                                          op0=ALU.mult, op1=ALU.add))
            dve.tensor_tensor(p_re[:, :], p_re[:, :], xT, ALU.mult)
            link(dve.tensor_tensor(p_im[:, :], p_im[:, :], xT, ALU.mult))
            dve.wait_ge(dx_ready, 1)
            dve.scalar_tensor_tensor(out=xr[:, :], in0=dx[:, :], scalar=V("mu_r"), in1=x_prev,
                                     op0=ALU.mult, op1=ALU.add).then_inc(mixin_ready, 1)
            dve.scalar_tensor_tensor(out=xk[:, :], in0=dx[:, :], scalar=V("mu_k"), in1=x_prev,
                                     op0=ALU.mult, op1=ALU.add).then_inc(mixin_ready, 1)
            dve.tensor_tensor_scan(turns[:, :], r_abs.to_broadcast([P, T]), p_re[:, :], in_re, ALU.mult, ALU.add)
            link(dve.tensor_tensor_scan(whole[:, :], r_abs.to_broadcast([P, T]), p_im[:, :], in_im,
                                        ALU.mult, ALU.add))
            dve.tensor_tensor(p_re[:, :], turns[:, :], cosT[:, :], ALU.mult)
            link(dve.tensor_tensor(p_im[:, :], whole[:, :], sinT[:, :], ALU.mult))
            link(dve.tensor_tensor(s_mix[:, :], p_re[:, :], p_im[:, :], ALU.subtract))
            for c in range(NCH):
                sl = slice(c * CH, (c + 1) * CH)
                dve.wait_ge(val_done, c + 1)
                dve.wait_ge(act_done, 2 * c + 1)
                dve.tensor_tensor(xr[:, sl], banks[4 + c % 2][:, :], sig[:, sl], ALU.mult).then_inc(val_free, 1)
                dve.wait_ge(val_free, c + 1)
                dve.tensor_tensor(s_mix[:, sl], s_mix[:, sl], xr[:, sl], ALU.add).then_inc(mix_ready, 1)
            for c in range(NCH):
                dve.wait_ge(back_done, c + 1)
                link(dve.tensor_tensor(X[:, TPC * c:TPC * (c + 1), :], X[:, TPC * c:TPC * (c + 1), :],
                                       banks[c][:, :].rearrange("p (i d) -> p i d", d=P), ALU.add))
                for i in range(TPC * c, TPC * (c + 1)):
                    last = dve.bn_stats(st6[:, i, :], X[:, i, :])
            link(last)
            for i in range(NT):
                last = dve.bn_aggr(mv[:, i, :], st6[:, i, :])
            link(last)
            dve.tensor_scalar(w2v[:, :], mv[:, :, 1], EPS, None, ALU.add).then_inc(var1_ready, 1)
            dve.wait_ge(rstd1_ready, 1)
            for i in range(NT):
                last = dve.tensor_scalar(S.xn1[:, i, :], X[:, i, :], mv[:, i, 0:1], rstd[:, i:i + 1],
                                         ALU.subtract, ALU.mult)
            link(dve.tensor_tensor(w2v[:, :], rstd[:, :], rstd[:, :], ALU.mult))
            link(dve.tensor_tensor(w2v[:, :], w2v[:, :], mv[:, :, 1], ALU.mult))
            link(dve.tensor_scalar(w2v[:, :], w2v[:, :], EPS, None, ALU.add))
            dve.sem_inc(w2_ready, 1)
            link(dve.tensor_tensor(S.res[:, :, :], X[:, :, :], S.xn1[:, :, :], ALU.add))
            dve.wait_ge(rstd2_ready, 1)
            for i in range(NT):
                dve.tensor_scalar(XN[:, i, :], S.xn1[:, i, :], rstd2[:, i:i + 1], None, ALU.mult).then_inc(xh_ready, 1)

        @block.tensor
        def _(pe):
            pe.wait_ge(ident_ready, 2)
            for i in range(NT):
                pe.wait_ge(xn_ready, i + 1)
                mm = pe.transpose(banks[i // TPC][:, P * (i % TPC):P * (i % TPC + 1)], XN[:, i, :], ident_w[:, :])
                if i % TPC == TPC - 1:
                    mm.then_inc(xT_psum, 1)
            pe.wait_ge(w_in, 16)
            pe.wait_ge(mixin_ready, 2)
            pe.wait_ge(xT_ready, NCH)

            def value(c):
                pe.wait_ge(sq_done, c + 1)
                if c >= 2:
                    pe.wait_ge(val_free, c - 1)
                pe.matmul(banks[4 + c % 2][:, :], W[:, 2, :], kact[:, c * CH:(c + 1) * CH],
                          start=True, stop=True).then_inc(val_done, 1)

            for c in range(NCH):
                if c >= 2:
                    pe.wait_ge(act_done, 2 * (c - 1))
                pe.matmul(banks[2 * (c % 2)][:, :], W[:, 0, :], xr[:, c * CH:(c + 1) * CH],
                          start=True, stop=True).then_inc(proj_done, 1)
                pe.matmul(banks[2 * (c % 2) + 1][:, :], W[:, 1, :], xk[:, c * CH:(c + 1) * CH],
                          start=True, stop=True).then_inc(proj_done, 1)
                if c >= 1:
                    value(c - 1)
            value(NCH - 1)
            pe.wait_ge(act_done, 2 * NCH)
            for c in range(NCH):
                pe.wait_ge(mix_ready, c + 1)
                for i in range(TPC * c, TPC * (c + 1)):
                    mm = pe.transpose(banks[c][:, P * (i % TPC):P * (i % TPC + 1)],
                                      s_mix[:, P * i:P * (i + 1)], ident_w[:, :])
                mm.then_inc(back_done, 1)
            pe.wait_ge(w2_ready, 1)
            for c in range(NCH):
                pe.wait_ge(xh_ready, TPC * (c + 1))
                for i in range(TPC):
                    mm = pe.transpose(banks[c][:, P * i:P * (i + 1)], XN[:, TPC * c + i, :], ident_w[:, :])
                mm.then_inc(xh_psum, 1)
                for i in range(TPC):
                    k = TPC - 1 - i
                    mm = pe.matmul(banks[4 + c][:, P * k:P * (k + 1)], XN[:, TPC * c + i, :], S.flip[:, :],
                                   start=True, stop=True)
                mm.then_inc(xh_psum, 1)



NG = 4
HG = NH // NG
DQ = 9 * HD
DM = DQ + 3
VW = 32


def attention_prep_stage(nc, S, dr):
    with ExitStack() as ctx:
        def sb(name, shape, dt=F32):
            return ctx.enter_context(nc.sbuf_tensor(name, shape, dt))

        def sem(name):
            return S.enter_sem(nc, name)

        W = sb("ap_w", [P, 3, P])
        bv = sb("ap_bv", [P, P])
        hn = sb("ap_hn", [P, T])
        rem = sb("ap_rem", [P, T])
        parts = sb("ap_parts", [P, 3, T], BF16)
        banks = S.banks
        w_in, dve_c = sem("ap_w_in"), sem("ap_dve_chain")
        ones_ready, ones_in = sem("ap_ones_ready"), sem("ap_ones_in")
        hn_ready, qk_psum, v_psum = sem("ap_hn"), sem("ap_qk_psum"), sem("ap_v_psum")
        f_ready, hi_ready, v_ready = sem("ap_f"), sem("ap_hi"), sem("ap_v")
        rem1_ready, parts_ready = sem("ap_rem1"), sem("ap_parts_ready")
        stored = [sem("ap_stored_q"), sem("ap_stored_k")]
        block = ctx.enter_context(nc.Block())

        def V(name):
            return S.vec[:, VCOL[name]:VCOL[name] + 1]

        @block.sync
        def _(sp):
            for i, n in enumerate(("wq", "wk", "wv")):
                sp.dma_start(W[:, i, :], dr[n]).then_inc(w_in, 16)
            sp.dma_start(bv[:, :], dr["bv"]).then_inc(w_in, 16)
            sp.wait_ge(ones_ready, 1)
            for g in range(NG):
                sp.dma_start(S.ks[DQ:DM, HG * g * T:HG * (g + 1) * T].rearrange("r (h t) -> r h t", t=T),
                             S.ones[0:3, :].unsqueeze(1).to_broadcast([3, HG, T])).then_inc(ones_in, 16)
            for w in range(2):
                sp.wait_ge(parts_ready, w + 1)
                sp.dma_start(S.qk_dram[w].rearrange("i f t -> f i t"), parts[:, :, :]).then_inc(stored[w], 16)
                sp.wait_ge(stored[w], 16)
            sp.wait_ge(ones_in, 16 * NG)

        @block.gpsimd
        def _(pool):
            pool.memset(S.ones[:, :], 1.0).then_inc(ones_ready, 1)

        @block.scalar
        def _(act):
            for w, bias in enumerate(("bq", "bk")):
                if w:
                    act.wait_ge(parts_ready, w)
                    act.wait_ge(stored[0], 16)
                for c in range(NCH):
                    act.wait_ge(qk_psum, NCH * w + c + 1)
                    act.activation(rem[:, c * CH:(c + 1) * CH], banks[4 * w + c][:, :], ACT.Identity,
                                   bias=V(bias)).then_inc(f_ready, 1)
                act.wait_ge(f_ready, NCH * (w + 1))
                act.activation(parts[:, 0, :], rem[:, :], ACT.Copy).then_inc(hi_ready, 1)

        @block.vector
        def _(dve):
            count = [0]

            def link(ins):
                count[0] += 1
                ins.then_inc(dve_c, 1)
                dve.wait_ge(dve_c, count[0])

            link(dve.tensor_copy(S.identb[:, :], S.ident[:, :]))
            dve.tensor_scalar(hn[:, :], S.xh[:, 0, :], V("ln1_g"), V("ln1_b"), ALU.mult, ALU.add).then_inc(hn_ready, 1)
            for w in range(2):
                dve.wait_ge(hi_ready, w + 1)
                link(dve.tensor_tensor(rem[:, :], rem[:, :], parts[:, 0, :], ALU.subtract))
                link(dve.tensor_copy(parts[:, 1, :], rem[:, :]))
                dve.tensor_tensor(parts[:, 2, :], rem[:, :], parts[:, 1, :], ALU.subtract).then_inc(parts_ready, 1)
            dve.wait_ge(w_in, 64)
            for c in range(NCH):
                dve.wait_ge(v_psum, c + 1)
                dve.tensor_tensor(S.v[:, TPC * c:TPC * (c + 1), :],
                                  banks[c][:, :].rearrange("p (i d) -> p i d", d=P),
                                  bv[:, :].unsqueeze(1).to_broadcast([P, TPC, P]), ALU.add).then_inc(v_ready, 1)

        @block.tensor
        def _(pe):
            pe.wait_ge(w_in, 64)
            pe.wait_ge(hn_ready, 1)
            for w in range(2):
                for c in range(NCH):
                    pe.matmul(banks[4 * w + c][:, :], W[:, w, :], hn[:, c * CH:(c + 1) * CH],
                              start=True, stop=True).then_inc(qk_psum, 1)
            pe.wait_ge(f_ready, NCH)
            for c in range(NCH):
                for i in range(TPC):
                    t = TPC * c + i
                    mm = pe.matmul(banks[c][:, P * i:P * (i + 1)], hn[:, P * t:P * (t + 1)], W[:, 2, :],
                                   start=True, stop=True)
                mm.then_inc(v_psum, 1)


def attention_stage(nc, S, dr):
    with ExitStack() as ctx:
        def sb(name, shape, dt=F32):
            return ctx.enter_context(nc.sbuf_tensor(name, shape, dt))

        def sem(name):
            return S.enter_sem(nc, name)

        vg = sb("at_vg", [P, NT, HG, VW])
        probs = sb("at_probs", [P, 2, 2, 2 * CH])
        osb = sb("at_osb", [P, CH])
        mpart = sb("at_mpart", [P, HG * NT, NCH])
        mx = sb("at_mx", [P, HG * NT])
        mrem = sb("at_mrem", [P, HG * NT])
        m3 = sb("at_m3", [P, 3, HG * NT], BF16)
        MR = 3 * HG * NT // 2
        mrow = sb("at_mrow", [MR, 2, P], BF16)
        rden = sb("at_rden", [P, TPC, HG])
        s_banks = [[S.banks[0], S.banks[1]], [S.banks[2], S.banks[3]]]
        s_pair = S.sc01, S.sc23
        o_bank, t_bank, m_bank = S.banks[4], S.banks[5], [S.banks[6], S.banks[7]]
        t_bf = t_bank[:, :].bitcast(BF16)

        q_in = [sem(f"at_q_in{g}") for g in range(NG)]
        k_in = [sem(f"at_k_in{g}") for g in range(NG)]
        mrow_in = sem("at_mrow_in")
        dve_c, act_c, pool_c = sem("at_dve_chain"), sem("at_act_chain"), sem("at_pool_chain")
        max_scores, max_free = sem("at_max_scores"), sem("at_max_free")
        m3_ready, mT_psum, mrow_ready = sem("at_m3"), sem("at_mT"), sem("at_mrow_ready")
        scores, scores_free = sem("at_scores"), sem("at_scores_free")
        probs_ready, probs_free = sem("at_probs_ready"), sem("at_probs_free")
        vg_ready = sem("at_vg_ready")
        o_copied, o_turned, o_normed = sem("at_o_copied"), sem("at_o_turned"), sem("at_o_normed")
        block = ctx.enter_context(nc.Block())
        HT = HG * T

        @block.sync
        def _(sp):
            for g in range(NG):
                for h in range(HG * g, HG * (g + 1)):
                    for i in range(3):
                        rows = slice(3 * HD * i, 3 * HD * (i + 1))
                        sp.dma_start(S.qs[rows, h * T:(h + 1) * T],
                                     S.qk_dram[0][i:i + 1, HD * h:HD * (h + 1), :].to_broadcast([3, HD, T]))\
                            .then_inc(q_in[g], 16)
                        sp.dma_start(S.ks[rows, h * T:(h + 1) * T],
                                     S.qk_dram[1][:, HD * h:HD * (h + 1), :]).then_inc(k_in[g], 16)

            def place_max(g, done):
                sp.wait_ge(mrow_ready, done)
                for r in range(3):
                    for j in range(HG):
                        k = r * HG + j
                        half, at = divmod(k * NT, MR)
                        sp.dma_start(S.qs[DQ + r:DQ + r + 1, bass.ds(g * HT + j * T, T)].rearrange("o (i p) -> o i p", p=P),
                                     mrow[at:at + NT, half, :]).then_inc(mrow_in, 16)

            place_max(0, 1)
            with sp.Fori(0, NG - 1) as g:
                place_max(g + 1, g + 2)
            sp.wait_ge(mrow_in, 16 * 3 * HG * NG)

        @block.gpsimd
        def _(pool):
            pool.memset(vg[:, :, :, :], 0.0).then_inc(pool_c, 1)
            pool.wait_ge(pool_c, 1)
            pool.memset(vg[:, :, :, HD:HD + 1], 1.0).then_inc(pool_c, 1)
            pool.wait_ge(pool_c, 2)
            with pool.Fori(0, NG) as g:
                pool.wait_ge(probs_free, g * (NCH * NT) + 2)
                pool.tensor_copy(vg[:, :, :, 0:HD],
                                 S.v[:, :, bass.ds(g * (HG * HD), HG * HD)].rearrange("p i (j d) -> p i j d", d=HD))\
                    .then_inc(vg_ready, 1)

        @block.scalar
        def _(act):
            with act.Fori(0, NG) as g:
                with act.Fori(0, NCH) as qc:
                    s = g * NCH + qc
                    for kt in range(NT):
                        act.wait_ge(probs_free, s * NT + (kt + 1))
                        for p in range(2):
                            act.wait_ge(scores, s * (2 * NT) + (2 * kt + p + 1))
                            act.activation(probs[:, kt % 2, p, :], s_pair[p][:, :], ACT.Exp,
                                           scale=float(HD) ** -0.5).then_inc(probs_ready, 1)

        @block.vector
        def _(dve):
            count = [0]

            def max_unit(unit, row):
                for kc in range(NCH):
                    dve.wait_ge(max_scores, unit * NCH + (kc + 1))
                    dve.reduce_max(mpart[:, row, kc:kc + 1], m_bank[kc % 2][:, :], AX.X).then_inc(max_free, 1)

            def max_group(n, first=False):
                base = n * 6
                dve.wait_ge(max_free, n * (HG * NT * NCH) + (HG * NT * NCH + 2))
                dve.tensor_reduce(mx[:, :], mpart[:, :, :], AX.X, ALU.max).then_inc(dve_c, 1)
                dve.wait_ge(dve_c, base + 1)
                dve.tensor_scalar(mrem[:, :], mx[:, :], -1.0, None, ALU.mult).then_inc(dve_c, 1)
                dve.wait_ge(dve_c, base + 2)
                dve.tensor_copy(m3[:, 0, :], mrem[:, :]).then_inc(dve_c, 1)
                dve.wait_ge(dve_c, base + 3)
                dve.tensor_tensor(mrem[:, :], mrem[:, :], m3[:, 0, :], ALU.subtract).then_inc(dve_c, 1)
                dve.wait_ge(dve_c, base + 4)
                dve.tensor_copy(m3[:, 1, :], mrem[:, :]).then_inc(dve_c, 1)
                dve.wait_ge(dve_c, base + 5)
                dve.tensor_tensor(m3[:, 2, :], mrem[:, :], m3[:, 1, :], ALU.subtract).then_inc(dve_c, 1)
                dve.wait_ge(dve_c, base + 6)
                dve.sem_inc(m3_ready, 1)
                if not first:
                    dve.wait_ge(mrow_in, n * (16 * 3 * HG))
                dve.wait_ge(mT_psum, n + 1)
                dve.tensor_copy(mrow[:, :, :], t_bf[0:MR, 0:2 * P].rearrange("r (a q) -> r a q", a=2))\
                    .then_inc(mrow_ready, 1)

            def finish(g, qc, s):
                dve.wait_ge(probs_free, (s + 1) * NT + 2)
                dve.tensor_copy(osb[:, :], o_bank[:, :]).then_inc(o_copied, 1)
                dve.wait_ge(o_turned, s + 1)
                turned = t_bank[:, :].rearrange("p (i j c) -> p i j c", i=TPC, c=VW)
                dve.reciprocal(rden[:, :, :], turned[:, :, :, HD]).then_inc(o_normed, 1)
                dve.wait_ge(o_normed, 2 * s + 1)
                dve.tensor_tensor(S.o[:, bass.ds(qc * TPC, TPC), bass.ds(g * (HG * HD), HG * HD)]
                                  .rearrange("p i (j d) -> p i j d", d=HD),
                                  turned[:, :, :, 0:HD], rden[:, :, :].unsqueeze(3).to_broadcast([P, TPC, HG, HD]),
                                  ALU.mult).then_inc(o_normed, 1)
                dve.wait_ge(o_normed, 2 * s + 2)

            dve.sem_inc(max_free, 2)
            dve.sem_inc(o_copied, 1)
            for j in range(HG):
                for kt in range(NT):
                    max_unit(NT * j + kt, NT * j + kt)
            max_group(0, first=True)
            with dve.Fori(0, NG - 1) as g:
                for qc in range(NCH):
                    for kt in range(NT):
                        max_unit(g * (HG * NT) + (HG * NT + NT * qc + kt), NT * qc + kt)
                    finish(g, qc, g * NCH + qc)
                max_group(g + 1)
            for qc in range(NCH):
                finish(NG - 1, qc, (NG - 1) * NCH + qc)

        @block.tensor
        def _(pe):
            def max_unit(unit, head, kt):
                for kc in range(NCH):
                    pe.wait_ge(max_free, unit * NCH + (kc + 1))
                    pe.matmul(m_bank[kc % 2][:, :], S.qs[0:DQ, bass.ds(head * T + kt * P, P)],
                              S.ks[0:DQ, bass.ds(head * T + kc * CH, CH)], start=True, stop=True)\
                        .then_inc(max_scores, 1)

            def turn_max(n):
                pe.wait_ge(m3_ready, n)
                flat = m3[:, :, :].rearrange("p r i -> p (r i)")
                for a in range(2):
                    mm = pe.transpose(t_bf[0:MR, P * a:P * (a + 1)], flat[:, MR * a:MR * (a + 1)], S.identb[:, :])
                mm.then_inc(mT_psum, 1)

            def score(g, qc, s, kt):
                for p in range(2):
                    pe.wait_ge(probs_ready, s * (2 * NT) + (2 * kt + p + 1))
                    for b in range(2):
                        j = 2 * p + b
                        mm = pe.matmul(s_banks[p][b], S.ks[0:DM, bass.ds(g * HT + (j * T + kt * P), P)],
                                       S.qs[0:DM, bass.ds(g * HT + (qc * CH + j * T), CH)], start=True, stop=True)
                    mm.then_inc(scores, 1)

            def weigh(s, kt):
                if kt == 0:
                    pe.wait_ge(o_copied, s + 1)
                pe.wait_ge(probs_ready, s * (2 * NT) + (2 * kt + 4))
                for j in range(HG):
                    mm = pe.matmul(o_bank[VW * j:VW * (j + 1), :], vg[:, kt, j, :],
                                   probs[:, kt % 2, j // 2, CH * (j % 2):CH * (j % 2 + 1)],
                                   start=(kt == 0), stop=(kt == NT - 1), tile_position=(0, VW * j))
                mm.then_inc(probs_free, 1)

            def turn_out(s):
                pe.wait_ge(o_copied, s + 2)
                for i in range(TPC):
                    mm = pe.transpose(t_bank[:, P * i:P * (i + 1)], osb[:, P * i:P * (i + 1)], S.ident[:, :])
                mm.then_inc(o_turned, 1)

            pe.sem_inc(probs_free, 2)
            pe.sem_inc(probs_ready, 2)
            pe.wait_ge(q_in[0], 16 * 3 * HG)
            pe.wait_ge(k_in[0], 16 * 3 * HG)
            for j in range(HG):
                for kt in range(NT):
                    max_unit(NT * j + kt, j, kt)
            turn_max(1)

            def group(g, qc, more):
                s = g * NCH + qc
                for kt in range(NT):
                    score(g, qc, s, kt)
                    if more:
                        max_unit(g * (HG * NT) + qc * NT + (HG * NT + kt), g * HG + HG + qc, kt)
                    if kt >= 1:
                        weigh(s, kt - 1)
                weigh(s, NT - 1)
                turn_out(s)

            with pe.Fori(0, NG - 1) as g:
                for n in range(1, NG):
                    pe.wait_ge(q_in[n], 16 * 3 * HG)
                    pe.wait_ge(k_in[n], 16 * 3 * HG)
                with pe.Fori(0, NCH) as qc:
                    pe.wait_ge(vg_ready, g + 1)
                    pe.wait_ge(mrow_in, g * (16 * 3 * HG) + 16 * 3 * HG)
                    group(g, qc, True)
                turn_max(g + 2)
            pe.wait_ge(vg_ready, NG)
            pe.wait_ge(mrow_in, NG * 16 * 3 * HG)
            with pe.Fori(0, NCH) as qc:
                group(NG - 1, qc, False)


def attention_out_stage(nc, S, dr):
    with ExitStack() as ctx:
        def sb(name, shape, dt=F32):
            return ctx.enter_context(nc.sbuf_tensor(name, shape, dt))

        def sem(name):
            return S.enter_sem(nc, name)

        W = sb("ao_w", [P, P])
        bo = sb("ao_bo", [P, P])
        oT = sb("ao_oT", [P, T])
        w_in, oT_psum, oT_ready, proj_done, dve_c = (sem("ao_w_in"), sem("ao_oT_psum"), sem("ao_oT_ready"),
                                                     sem("ao_proj"), sem("ao_dve_chain"))
        banks = S.banks
        block = ctx.enter_context(nc.Block())

        @block.sync
        def _(sp):
            sp.dma_start(W[:, :], dr["wo"]).then_inc(w_in, 16)
            sp.dma_start(bo[:, :], dr["bo"]).then_inc(w_in, 16)
            sp.wait_ge(w_in, 32)

        @block.scalar
        def _(act):
            for c in range(NCH):
                act.wait_ge(oT_psum, c + 1)
                act.activation(oT[:, c * CH:(c + 1) * CH], banks[c][:, :], ACT.Copy).then_inc(oT_ready, 1)

        @block.tensor
        def _(pe):
            for c in range(NCH):
                for i in range(TPC):
                    mm = pe.transpose(banks[c][:, P * i:P * (i + 1)], S.o[:, TPC * c + i, :], S.ident[:, :])
                mm.then_inc(oT_psum, 1)
            pe.wait_ge(w_in, 32)
            for c in range(NCH):
                pe.wait_ge(oT_ready, c + 1)
                for i in range(TPC):
                    t = TPC * c + i
                    mm = pe.matmul(banks[4 + c][:, P * i:P * (i + 1)], oT[:, P * t:P * (t + 1)], W[:, :],
                                   start=True, stop=True)
                mm.then_inc(proj_done, 1)

        @block.vector
        def _(dve):
            dve.wait_ge(w_in, 32)
            for c in range(NCH):
                x2 = S.xn1[:, TPC * c:TPC * (c + 1), :]
                r = S.res[:, TPC * c:TPC * (c + 1), :]
                dve.wait_ge(proj_done, c + 1)
                dve.tensor_tensor(x2, x2, banks[4 + c][:, :].rearrange("p (i d) -> p i d", d=P), ALU.add).then_inc(dve_c, 1)
                dve.wait_ge(dve_c, 3 * c + 1)
                dve.tensor_tensor(x2, x2, bo[:, :].unsqueeze(1).to_broadcast([P, TPC, P]), ALU.add).then_inc(dve_c, 1)
                dve.wait_ge(dve_c, 3 * c + 2)
                dve.tensor_tensor(r, r, x2, ALU.add).then_inc(dve_c, 1)


def attention(nc, S, dr):
    with ExitStack() as ctx:
        S.qk_dram = [nc.dram_tensor(f"{n}_parts", [3, P, T], BF16).ap() for n in "qk"]
        S.v = ctx.enter_context(nc.sbuf_tensor("at_v", [P, NT, P], F32))
        S.identb = ctx.enter_context(nc.sbuf_tensor("identb", [P, P], BF16))
        with ExitStack() as big:
            S.qs = big.enter_context(nc.sbuf_tensor("at_qs", [P, NH * T], BF16))
            S.ks = big.enter_context(nc.sbuf_tensor("at_ks", [P, NH * T], BF16))
            with ExitStack() as c2:
                S.ones = c2.enter_context(nc.sbuf_tensor("at_ones", [3, T], BF16))
                attention_prep_stage(nc, S, dr)
                S.end_stage(nc)
            with ExitStack() as c2:
                S.o = S.v
                attention_stage(nc, S, dr)
                S.end_stage(nc)
        attention_out_stage(nc, S, dr)
        S.end_stage(nc)


BC = 2 * NS
BC3 = 3 * BC


def mamba_prep_stage(nc, S, dr, d):
    name = "fb"[d]
    with ExitStack() as ctx:
        def sb(n, shape, dt=F32):
            return ctx.enter_context(nc.sbuf_tensor(f"mp{name}_{n}", shape, dt))

        def sem(n):
            return S.enter_sem(nc, f"mp{name}_{n}")

        w_in_sb = sb("w_in", [P, 2 * DI])
        w_x = sb("w_x", [P, NB, BC3 + DR])
        w_dt = sb("w_dt", [P, DI])
        xm = sb("xm", [P, T])
        up = sb("up", [P, NB, T + KC - 1])
        rem = xm
        soft = up
        mid = sb("mid", [P, T], BF16)
        dtr = sb("dtr", [P, T])
        banks, lo4, hi4 = S.banks, S.psum[:, 0:T], S.psum[:, T:2 * T]
        w_load = sem("w_load")
        pad_ready, xm_ready, dve_c, act_c, pool_c = sem("pad"), sem("xm_r"), sem("dve_chain"), sem("act_chain"), sem("pool_chain")
        u_psum, u_out, z_psum, z_out = sem("u_psum"), sem("u_out"), sem("z_psum"), sem("z_out")
        conv_ready, u_ready = sem("conv"), sem("u_ready")
        xd_psum, hi_ready, dtr_ready, split_done = sem("xd_psum"), sem("hi"), sem("dtr_r"), sem("split")
        dt_psum, relu_ready, soft_ready, aexp_ready = sem("dt_psum"), sem("relu"), sem("soft"), sem("aexp")
        exp_ready = sem("exp_ready")
        block = ctx.enter_context(nc.Block())

        def V(n):
            return S.vec[:, VCOL[n]:VCOL[n] + 1]

        @block.sync
        def _(sp):
            sp.dma_start(w_in_sb[:, :], dr["w_in"][d]).then_inc(w_load, 16)
            sp.dma_start(w_x[:, :, :], dr["w_x"][d].rearrange("(b p) e -> p b e", p=P)).then_inc(w_load, 16)
            sp.dma_start(w_dt[BC3:BC3 + DR, :], dr["w_dt"][d]).then_inc(w_load, 16)
            sp.wait_ge(w_load, 48)

        @block.gpsimd
        def _(pool):
            pool.memset(up[:, :, 0:KC - 1], 0.0).then_inc(pad_ready, 1)
            if d == 0:
                pool.memset(S.sel[:, :], 0.0).then_inc(pool_c, 1)
                sel = S.sel[:, :].rearrange("k (j m) -> k j m", m=P)
                for r in range(3):
                    pool.wait_ge(pool_c, r + 1)
                    pool.affine_select(out=sel, in_=sel, compare_op=ALU.not_equal, fill=1.0, base=-BC * r,
                                       pattern=[[-1, BC], [0, P]], channel_multiplier=1).then_inc(pool_c, 1)

        @block.scalar
        def _(act):
            for b in range(NB):
                act.wait_ge(u_psum, b + 1)
                act.activation(up[:, b, KC - 1:KC - 1 + T], (lo4, hi4)[b], ACT.Copy).then_inc(u_out, 1)
            for b in range(NB):
                act.wait_ge(z_psum, b + 1)
                act.activation(S.zs[:, b, :], (lo4, hi4)[b], ACT.Silu).then_inc(z_out, 1)
            for b in range(NB):
                act.wait_ge(conv_ready, b + 1)
                act.activation(S.u[:, b, :], S.dt[:, b, :], ACT.Silu).then_inc(u_ready, 1)
            act.wait_ge(xd_psum, 1)
            act.activation(dtr[BC3:BC3 + DR, :], S.psum[BC3:BC3 + DR, 0:T], ACT.Copy).then_inc(dtr_ready, 1)
            act.wait_ge(dtr_ready, 1)
            act.activation(S.bc[:, :], S.psum[0:BC3, 0:T], ACT.Copy).then_inc(hi_ready, 1)
            a0 = VCOL[f"{name}_Alog0_0"]
            act.activation(S.aneg[:, :], S.vec[:, a0:a0 + NB * NS], ACT.Exp).then_inc(aexp_ready, 1)
            for b in range(NB):
                act.wait_ge(dt_psum, b + 1)
                sf = soft[:, b, 0:T]
                act.activation(sf, (hi4, lo4)[b], ACT.Abs, bias=V(f"{name}_bdt{b}")).then_inc(act_c, 1)
            for b in range(NB):
                sf = soft[:, b, 0:T]
                act.wait_ge(act_c, b + 1)
                act.activation(sf, sf, ACT.Exp, scale=-1.0).then_inc(exp_ready, 1)
            for b in range(NB):
                sf = soft[:, b, 0:T]
                act.wait_ge(exp_ready, b + 1)
                act.activation(sf, sf, ACT.Ln, bias=1.0).then_inc(soft_ready, 1)

        @block.vector
        def _(dve):
            count = [0]

            def link(ins):
                count[0] += 1
                ins.then_inc(dve_c, 1)
                dve.wait_ge(dve_c, count[0])

            dve.tensor_scalar(xm[:, :], S.xh[:, d, :], V("norm_g"), V("norm_b"), ALU.mult, ALU.add).then_inc(xm_ready, 1)
            for b in range(NB):
                link(dve.tensor_scalar(S.diag[:, b, :], S.ident[:, :], V(f"{name}_D{b}"), None, ALU.mult))
            dve.wait_ge(pad_ready, 1)
            for b in range(NB):
                dve.wait_ge(u_out, b + 1)
                acc = S.dt[:, b, :]
                link(dve.tensor_scalar(acc, up[:, b, 0:T], V(f"{name}_convw{b}0"), V(f"{name}_convb{b}"),
                                       ALU.mult, ALU.add))
                for k in range(1, KC):
                    ins = dve.scalar_tensor_tensor(out=acc, in0=up[:, b, k:k + T], scalar=V(f"{name}_convw{b}{k}"),
                                                   in1=acc, op0=ALU.mult, op1=ALU.add)
                    if k < KC - 1:
                        link(ins)
                    else:
                        ins.then_inc(conv_ready, 1)
            dve.wait_ge(hi_ready, 1)
            link(dve.tensor_tensor(rem[0:BC3, :], S.psum[0:BC3, 0:T], S.bc[:, :], ALU.subtract))
            dve.tensor_copy(S.bc[BC:2 * BC, :], rem[BC:2 * BC, :])
            link(dve.tensor_copy(mid[2 * BC:BC3, :], rem[2 * BC:BC3, :]))
            dve.tensor_tensor(S.bc[2 * BC:BC3, :], rem[2 * BC:BC3, :], mid[2 * BC:BC3, :],
                              ALU.subtract).then_inc(split_done, 1)
            dve.wait_ge(aexp_ready, 1)
            link(dve.tensor_scalar(S.aneg[:, :], S.aneg[:, :], -1.0, None, ALU.mult))
            for b in range(NB):
                dve.wait_ge(act_c, b + 1)
                dve.tensor_scalar(S.dt[:, b, :], (hi4, lo4)[b], V(f"{name}_bdt{b}"), 0.0, ALU.add,
                                  ALU.max).then_inc(relu_ready, 1)
            for b in range(NB):
                dve.wait_ge(relu_ready, b + 1)
                dve.wait_ge(soft_ready, b + 1)
                link(dve.tensor_tensor(S.dt[:, b, :], S.dt[:, b, :], soft[:, b, 0:T], ALU.add))
                link(dve.tensor_tensor(S.dtu[:, b, :], S.dt[:, b, :], S.u[:, b, :], ALU.mult))

        @block.tensor
        def _(pe):
            pe.wait_ge(w_load, 48)
            pe.wait_ge(xm_ready, 1)
            for which, done, free in ((0, u_psum, None), (1, z_psum, u_out)):
                for b in range(NB):
                    if free is not None:
                        pe.wait_ge(free, b + 1)
                    for c in range(NCH):
                        col = DI * which + P * b
                        mm = pe.matmul(banks[4 * b + c], w_in_sb[:, col:col + P], xm[:, c * CH:(c + 1) * CH],
                                       start=True, stop=True)
                    mm.then_inc(done, 1)
            pe.wait_ge(z_out, 1)
            pe.wait_ge(u_ready, NB)
            for c in range(NCH):
                for b in range(NB):
                    mm = pe.matmul(banks[c][0:BC3 + DR, :], w_x[:, b, :], S.u[:, b, c * CH:(c + 1) * CH],
                                   start=(b == 0), stop=(b == NB - 1))
            mm.then_inc(xd_psum, 1)
            pe.wait_ge(dtr_ready, 1)
            pe.wait_ge(z_out, NB)
            for b in range(NB):
                if b:
                    pe.wait_ge(split_done, 1)
                for c in range(NCH):
                    mm = pe.matmul(banks[(4, 0)[b] + c], w_dt[BC3:BC3 + DR, P * b:P * (b + 1)],
                                   dtr[BC3:BC3 + DR, c * CH:(c + 1) * CH], start=True, stop=True)
                mm.then_inc(dt_psum, 1)


def mamba_scan_stage(nc, S, dr, d):
    name = "fb"[d]
    with ExitStack() as ctx:
        def sb(n, shape, dt=F32):
            return ctx.enter_context(nc.sbuf_tensor(f"ms{name}_{n}", shape, dt))

        def sem(n):
            return S.enter_sem(nc, f"ms{name}_{n}")

        decay = sb("decay", [P, 2, NB, CH])
        inject = sb("inject", [P, 2, NB, CH])
        crow = sb("crow", [P, 2, CH])
        hc = sb("hc", [P, 2, NB, CH])
        b_bank, c_bank, y_bank = S.banks[0:2], S.banks[2:4], S.banks[4:6]
        b_spread, b_free, c_spread, c_copied = sem("b_spread"), sem("b_free"), sem("c_spread"), sem("c_copied")
        decay_ready, scanned, weighted, summed = sem("decay_r"), sem("scanned"), sem("weighted"), sem("summed")
        y_free, first_ready, turns = sem("y_free"), sem("first_ready"), sem("turns")
        WC = NB * NS + 2 * NB
        block = ctx.enter_context(nc.Block())

        @block.scalar
        def _(act):
            act.sem_inc(c_copied, 2)
            with act.Fori(0, NCH) as c:
                for n in range(NS):
                    act.wait_ge(scanned, c * (NB * NS) + NB * (n + 1))
                    act.sem_inc(turns, 1)
                    for b in range(NB):
                        act.activation(decay[:, n % 2, b, :], S.dt[:, b, bass.ds(c * CH, CH)], ACT.Exp,
                                       scale=S.aneg[:, NS * b + n:NS * b + n + 1]).then_inc(decay_ready, 1)
                    act.wait_ge(c_spread, c * NS + (n + 1))
                    act.wait_ge(weighted, c * (NB * NS) + (NB * (n - 1) + WC))
                    act.activation(crow[:, n % 2, :], c_bank[n % 2], ACT.Copy).then_inc(c_copied, 1)

        @block.vector
        def _(dve):
            dve.sem_inc(scanned, 2 * NB)
            dve.sem_inc(b_free, 2 * NB)
            dve.sem_inc(y_free, NB)
            dve.wait_ge(first_ready, 1)
            with dve.Fori(0, NCH) as c:
                for n in range(NS):
                    dve.wait_ge(b_spread, c * NS + (n + 1))
                    dve.wait_ge(scanned, c * (NB * NS) + NB * (n + 1))
                    for b in range(NB):
                        dve.tensor_tensor(inject[:, n % 2, b, :], S.dtu[:, b, bass.ds(c * CH, CH)], b_bank[n % 2],
                                          ALU.mult).then_inc(b_free, 1)
                    for b in range(NB):
                        step = NB * n + b
                        dve.wait_ge(decay_ready, c * (NB * NS) + (step + 1))
                        dve.wait_ge(b_free, c * (NB * NS) + (step + 1 + 2 * NB))
                        dve.wait_ge(weighted, c * (NB * NS) + (step + 1 + 2 * NB))
                        dve.tensor_tensor_scan(S.h[:, b, n, :], decay[:, n % 2, b, :], inject[:, n % 2, b, :],
                                               S.h[:, b, n, CH - 1:CH], ALU.mult, ALU.add).then_inc(scanned, 1)
                dve.wait_ge(summed, c * NS + (NS + 2))
                for b in range(NB):
                    gated = S.zs[:, b, bass.ds(c * CH, CH)]
                    dve.tensor_tensor(gated, gated, y_bank[b], ALU.mult).then_inc(y_free, 1)

        @block.gpsimd
        def _(pool):
            pool.sem_inc(weighted, WC)
            pool.memset(S.h[:, :, :, CH - 1:CH], 0.0).then_inc(first_ready, 1)
            with pool.Fori(0, NCH) as c:
                for n in range(NS):
                    pool.wait_ge(c_copied, c * NS + (n + 3))
                    pool.wait_ge(summed, c * NS + (n + 1))
                    for b in range(NB):
                        pool.wait_ge(scanned, c * (NB * NS) + (NB * n + b + 1 + 2 * NB))
                        pool.tensor_tensor(hc[:, n % 2, b, :], S.h[:, b, n, :], crow[:, n % 2, :],
                                           ALU.mult).then_inc(weighted, 1)

        @block.tensor
        def _(pe):
            pe.sem_inc(summed, 2)

            def spread(c, n):
                cols = bass.ds(c * CH, CH)
                pe.wait_ge(b_free, c * (NB * NS) + NB * (n + 1))
                pe.matmul(b_bank[n % 2], S.sel[:, P * n:P * (n + 1)], S.bc[:, cols],
                          start=True, stop=True).then_inc(b_spread, 1)
                pe.wait_ge(c_copied, c * NS + (n + 1))
                pe.matmul(c_bank[n % 2], S.sel[:, P * (NS + n):P * (NS + n + 1)], S.bc[:, cols],
                          start=True, stop=True).then_inc(c_spread, 1)

            with pe.Fori(0, NCH) as c:
                spread(c, 0)
                spread(c, 1)
                for b in range(NB):
                    pe.wait_ge(y_free, c * NB + (b + 1))
                    pe.matmul(y_bank[b], S.diag[:, b, :], S.u[:, b, bass.ds(c * CH, CH)],
                              start=True, stop=False)
                for n in range(NS):
                    for b in range(NB):
                        pe.wait_ge(weighted, c * (NB * NS) + (NB * n + b + 1 + WC))
                        mm = pe.matmul(y_bank[b], S.ident[:, :], hc[:, n % 2, b, :],
                                       start=False, stop=(n == NS - 1))
                    mm.then_inc(summed, 1)
                    if n + 2 < NS:
                        spread(c, n + 2)


def mamba_out_stage(nc, S, dr, d):
    name = "fb"[d]
    with ExitStack() as ctx:
        def sem(n):
            return S.enter_sem(nc, f"mo{name}_{n}")

        w_out = ctx.enter_context(nc.sbuf_tensor(f"mo{name}_w", [P, NB, P], F32))
        nat = ctx.enter_context(nc.sbuf_tensor(f"mo{name}_nat", [P, NCH, CH], F32))
        w_load, out_psum, nat_ready, turned, added = sem("w_load"), sem("psum"), sem("nat_ready"), sem("turned"), sem("added")
        banks = S.banks
        block = ctx.enter_context(nc.Block())

        @block.sync
        def _(sp):
            sp.dma_start(w_out[:, :, :], dr["w_out"][d].rearrange("(b p) e -> p b e", p=P)).then_inc(w_load, 16)
            sp.wait_ge(w_load, 16)

        @block.tensor
        def _(pe):
            pe.wait_ge(w_load, 16)
            for c in range(NCH):
                for i in range(TPC):
                    t = TPC * c + i
                    for b in range(NB):
                        mm = pe.matmul(banks[c][:, P * i:P * (i + 1)], S.zs[:, b, P * t:P * (t + 1)], w_out[:, b, :],
                                       start=(b == 0), stop=(b == NB - 1))
                mm.then_inc(out_psum, 1)
            if d:
                for c in range(NCH):
                    pe.wait_ge(nat_ready, c + 1)
                    pe.matmul(banks[4 + c], S.flip[:, :], nat[:, c, :], start=True, stop=True).then_inc(turned, 1)

        @block.scalar
        def _(act):
            if d:
                for c in range(NCH):
                    act.wait_ge(out_psum, c + 1)
                    act.activation(nat[:, c, :], banks[c], ACT.Copy).then_inc(nat_ready, 1)

        @block.vector
        def _(dve):
            for c in range(NCH):
                if d == 0:
                    dve.wait_ge(out_psum, c + 1)
                    r = S.res[:, TPC * c:TPC * (c + 1), :]
                    dve.tensor_tensor(r, r, banks[c].rearrange("p (i d) -> p i d", d=P), ALU.add).then_inc(added, 1)
                else:
                    dve.wait_ge(turned, c + 1)
                    for i in range(TPC):
                        r = S.res[:, NT - 1 - (TPC * c + i), :]
                        dve.tensor_tensor(r, r, banks[4 + c][:, P * i:P * (i + 1)], ALU.add).then_inc(added, 1)


def mamba(nc, S, dr):
    with ExitStack() as ctx:
        def sb(n, shape, dt=F32):
            return ctx.enter_context(nc.sbuf_tensor(f"m_{n}", shape, dt))

        S.u, S.zs, S.dt, S.dtu = (sb(n, [P, NB, T]) for n in ("u", "zs", "dt", "dtu"))
        S.bc = sb("bc", [BC3, T], BF16)
        S.sel = sb("sel", [BC3, BC * P], BF16)
        S.aneg = sb("aneg", [P, NB * NS])
        S.diag = sb("diag", [P, NB, P])
        for d in range(2):
            mamba_prep_stage(nc, S, dr, d)
            S.end_stage(nc)
            with ExitStack() as c2:
                S.h = c2.enter_context(nc.sbuf_tensor(f"m_h{d}", [P, NB, NS, CH], F32))
                mamba_scan_stage(nc, S, dr, d)
                S.end_stage(nc)
            mamba_out_stage(nc, S, dr, d)
            S.end_stage(nc)


def moe_prep_stage(nc, S, dr):
    with ExitStack() as ctx:
        def sb(n, shape, dt=F32):
            return ctx.enter_context(nc.sbuf_tensor(f"xp_{n}", shape, dt))

        def sem(n):
            return S.enter_sem(nc, f"xp_{n}")

        st6, mv = sb("st6", [P, NT, 6]), sb("mv", [P, NT, 2])
        lnv, rstd = sb("lnv", [P, NT]), sb("rstd", [P, NT])
        xn = sb("xn", [P, NT, P])
        gw, gb, b2 = sb("gw", [P, NE]), sb("gb", [P, NE]), sb("b2", [NE, P])
        rank_i, rank = sb("rank_i", [P, NE], I32), sb("rank", [P, NE])
        lg, top, pick = sb("lg", [P, NT, NE]), sb("top", [P, NT]), sb("pick", [P, NT, NE])
        ohT = sb("ohT", [NE, T])
        banks = S.banks
        w_load, rank_ready, dve_c, act_c = sem("w_load"), sem("rank"), sem("dve_chain"), sem("act_chain")
        var_ready, rstd_ready, xn_ready, xn_psum, hn_ready = sem("var"), sem("rstd"), sem("xn_r"), sem("xn_psum"), sem("hn_r")
        lg_psum, oh_ready, ohT_psum, ohT_ready, b2_psum = sem("lg_psum"), sem("oh_r"), sem("ohT_psum"), sem("ohT_r"), sem("b2_psum")
        block = ctx.enter_context(nc.Block())

        def V(n):
            return S.vec[:, VCOL[n]:VCOL[n] + 1]

        @block.sync
        def _(sp):
            sp.dma_start(gw[:, :], dr["gate_w"]).then_inc(w_load, 16)
            sp.dma_start(gb[:, :], dr["gate_b"]).then_inc(w_load, 16)
            sp.dma_start(b2[:, :], dr["b2"]).then_inc(w_load, 16)
            sp.wait_ge(w_load, 48)

        @block.gpsimd
        def _(pool):
            pool.iota(rank_i[:, :], pattern=[[-1, NE]], base=NE, channel_multiplier=0).then_inc(rank_ready, 1)

        @block.scalar
        def _(act):
            act.wait_ge(var_ready, 1)
            act.activation(lnv[:, :], lnv[:, :], ACT.Ln).then_inc(act_c, 1)
            act.wait_ge(act_c, 1)
            act.activation(rstd[:, :], lnv[:, :], ACT.Exp, scale=-0.5).then_inc(rstd_ready, 1)
            for c in range(NCH):
                act.wait_ge(xn_psum, c + 1)
                act.activation(S.hn2[:, c * CH:(c + 1) * CH], banks[c], ACT.Identity, bias=V("ln2_b"),
                               scale=V("ln2_g")).then_inc(hn_ready, 1)
            for c in range(NCH):
                act.wait_ge(ohT_psum, c + 1)
                act.activation(ohT[:, c * CH:(c + 1) * CH], banks[c][0:NE, :], ACT.Copy).then_inc(ohT_ready, 1)

        @block.vector
        def _(dve):
            count = [0]

            def link(ins):
                count[0] += 1
                ins.then_inc(dve_c, 1)
                dve.wait_ge(dve_c, count[0])

            for i in range(NT):
                last = dve.bn_stats(st6[:, i, :], S.xn1[:, i, :])
            link(last)
            for i in range(NT):
                last = dve.bn_aggr(mv[:, i, :], st6[:, i, :])
            link(last)
            dve.tensor_scalar(lnv[:, :], mv[:, :, 1], EPS, None, ALU.add).then_inc(var_ready, 1)
            dve.wait_ge(rstd_ready, 1)
            for i in range(NT):
                dve.tensor_scalar(xn[:, i, :], S.xn1[:, i, :], mv[:, i, 0:1], rstd[:, i:i + 1],
                                  ALU.subtract, ALU.mult).then_inc(xn_ready, 1)
            dve.wait_ge(rank_ready, 1)
            link(dve.tensor_copy(rank[:, :], rank_i[:, :]))
            dve.wait_ge(w_load, 48)
            dve.wait_ge(lg_psum, 1)
            link(dve.tensor_tensor(lg[:, :, :], banks[4][:, 0:NT * NE].rearrange("p (i e) -> p i e", e=NE),
                                   gb[:, :].unsqueeze(1).to_broadcast([P, NT, NE]), ALU.add))
            link(dve.tensor_reduce(top[:, :], lg[:, :, :], AX.X, ALU.max))
            link(dve.tensor_tensor(pick[:, :, :], lg[:, :, :], top[:, :].unsqueeze(2).to_broadcast([P, NT, NE]),
                                   ALU.is_ge))
            link(dve.tensor_tensor(pick[:, :, :], pick[:, :, :], rank[:, :].unsqueeze(1).to_broadcast([P, NT, NE]),
                                   ALU.mult))
            link(dve.tensor_reduce(top[:, :], pick[:, :, :], AX.X, ALU.max))
            dve.tensor_tensor(S.oh[:, :, :], pick[:, :, :], top[:, :].unsqueeze(2).to_broadcast([P, NT, NE]),
                              ALU.is_equal).then_inc(oh_ready, 1)
            for c in range(NCH):
                dve.wait_ge(b2_psum, c + 1)
                r = S.res[:, TPC * c:TPC * (c + 1), :]
                dve.tensor_tensor(r, r, banks[4 + c].rearrange("p (i d) -> p i d", d=P), ALU.add).then_inc(dve_c, 1)

        @block.tensor
        def _(pe):
            for c in range(NCH):
                pe.wait_ge(xn_ready, TPC * (c + 1))
                for i in range(TPC):
                    mm = pe.transpose(banks[c][:, P * i:P * (i + 1)], xn[:, TPC * c + i, :], S.ident[:, :])
                mm.then_inc(xn_psum, 1)
            pe.wait_ge(w_load, 48)
            pe.wait_ge(hn_ready, NCH)
            for t in range(NT):
                mm = pe.matmul(banks[4][:, NE * t:NE * (t + 1)], S.hn2[:, P * t:P * (t + 1)], gw[:, :],
                               start=True, stop=True)
            mm.then_inc(lg_psum, 1)
            pe.wait_ge(oh_ready, 1)
            for c in range(NCH):
                for i in range(TPC):
                    mm = pe.transpose(banks[c][0:NE, P * i:P * (i + 1)], S.oh[:, TPC * c + i, :], S.ident[:, :])
                mm.then_inc(ohT_psum, 1)
            for c in range(NCH):
                pe.wait_ge(ohT_ready, c + 1)
                for i in range(TPC):
                    t = TPC * c + i
                    mm = pe.matmul(banks[4 + c][:, P * i:P * (i + 1)], ohT[:, P * t:P * (t + 1)], b2[:, :],
                                   start=True, stop=True)
                mm.then_inc(b2_psum, 1)


def moe_stage(nc, S, dr):
    with ExitStack() as ctx:
        def sb(n, shape, dt=F32):
            return ctx.enter_context(nc.sbuf_tensor(f"xe_{n}", shape, dt))

        def sem(n):
            return S.enter_sem(nc, f"xe_{n}")

        w1, w2, b1 = sb("w1", [P, 2, NF]), sb("w2", [P, 2, NFB, P]), sb("b1", [P, 2, NFB])
        mid = sb("mid", [P, 2, NFB, CH])
        banks = S.banks
        w_load = [sem("w_load0"), sem("w_load1")]
        mid_psum, mid_ready, y_psum, added = sem("mid_psum"), sem("mid_ready"), sem("y_psum"), sem("added")
        block = ctx.enter_context(nc.Block())
        NP = NE // 2

        @block.sync
        def _(sp):
            def load(e, par):
                sp.dma_start(w1[:, par, :], dr["w1"][bass.ds(e, 1)].rearrange("o h f -> h (o f)")).then_inc(w_load[par], 16)
                sp.dma_start(w2[:, par, :, :], dr["w2"][bass.ds(e, 1)].rearrange("o (b p) h -> p (o b) h", p=P))\
                    .then_inc(w_load[par], 16)
                sp.dma_start(b1[:, par, :], dr["b1"][bass.ds(e, 1)].rearrange("o p b -> p (o b)")).then_inc(w_load[par], 16)

            load(0, 0)
            load(1, 1)
            with sp.Fori(0, NP - 1) as ep:
                for par in range(2):
                    sp.wait_ge(y_psum, ep * (2 * NCH) + (NCH * (par + 1) + 2))
                    load(ep * 2 + (2 + par), par)

        @block.scalar
        def _(act):
            with act.Fori(0, NP) as ep:
                for par in range(2):
                    for c in range(NCH):
                        step = NCH * par + c
                        act.wait_ge(y_psum, ep * (2 * NCH) + (step + 1))
                        for f in range(NFB):
                            act.wait_ge(mid_psum, ep * (2 * NCH * NFB) + (NFB * step + f + 1))
                            act.activation(mid[:, c % 2, f, :], banks[f], ACT.Relu,
                                           bias=b1[:, par, f:f + 1]).then_inc(mid_ready, 1)

        @block.vector
        def _(dve):
            dve.sem_inc(added, 2)
            with dve.Fori(0, NP) as ep:
                for par in range(2):
                    for c in range(NCH):
                        step = NCH * par + c
                        dve.wait_ge(y_psum, ep * (2 * NCH) + (step + 3))
                        for i in range(TPC):
                            t = TPC * c + i
                            ins = dve.scalar_tensor_tensor(
                                out=S.res[:, t, :], in0=banks[4 + c % 2][:, P * i:P * (i + 1)],
                                scalar=S.oh[:, t, bass.ds(ep * 2 + par, 1)], in1=S.res[:, t, :],
                                op0=ALU.mult, op1=ALU.add)
                        ins.then_inc(added, 1)
                        dve.wait_ge(added, ep * (2 * NCH) + (step + 3))

        @block.tensor
        def _(pe):
            pe.sem_inc(mid_ready, NFB)
            pe.sem_inc(y_psum, 2)

            def hidden(ep, par, c):
                step = NCH * par + c
                for f in range(NFB):
                    pe.wait_ge(mid_ready, ep * (2 * NCH * NFB) + (NFB * step + f + 1))
                    pe.matmul(banks[f], w1[:, par, P * f:P * (f + 1)], S.hn2[:, c * CH:(c + 1) * CH],
                              start=True, stop=True).then_inc(mid_psum, 1)

            def output(ep, par, c):
                step = NCH * par + c
                pe.wait_ge(added, ep * (2 * NCH) + (step + 1))
                pe.wait_ge(mid_ready, ep * (2 * NCH * NFB) + (NFB * (step + 2)))
                for i in range(TPC):
                    for f in range(NFB):
                        mm = pe.matmul(banks[4 + c % 2][:, P * i:P * (i + 1)], mid[:, c % 2, f, P * i:P * (i + 1)],
                                       w2[:, par, f, :], start=(f == 0), stop=(f == NFB - 1))
                mm.then_inc(y_psum, 1)

            with pe.Fori(0, NP) as ep:
                for par in range(2):
                    for c in range(NCH):
                        if c == 0:
                            pe.wait_ge(w_load[par], ep * 48 + 48)
                        hidden(ep, par, c)
                        if par or c:
                            output(ep, *divmod(NCH * par + c - 1, NCH))
                output(ep, 1, NCH - 1)


def moe(nc, S, dr):
    with ExitStack() as ctx:
        S.hn2 = ctx.enter_context(nc.sbuf_tensor("x_hn2", [P, T], F32))
        S.oh = ctx.enter_context(nc.sbuf_tensor("x_oh", [P, NT, NE], F32))
        moe_prep_stage(nc, S, dr)
        S.end_stage(nc)
        moe_stage(nc, S, dr)
        S.end_stage(nc)



def build(nc, dr, out, upto=9):
    with ExitStack() as ctx:
        S = Shared()
        S.sems = []
        S.ident = ctx.enter_context(nc.sbuf_tensor("ident", [P, P], F32))
        S.flip = ctx.enter_context(nc.sbuf_tensor("flip", [P, P], F32))
        S.vec = ctx.enter_context(nc.sbuf_tensor("vec", [P, NV], F32))
        S.res = ctx.enter_context(nc.sbuf_tensor("res", [P, NT, P], F32))
        S.xn1 = ctx.enter_context(nc.sbuf_tensor("xn1", [P, NT, P], F32))
        S.xh = ctx.enter_context(nc.sbuf_tensor("xh", [P, 2, T], F32))
        psum = ctx.enter_context(nc.psum_tensor("psum", [P, 8 * CH], F32))
        S.psum = psum
        S.banks = [psum[:, i * CH:(i + 1) * CH] for i in range(8)]
        S.sc01, S.sc23 = psum[:, 0:2 * CH], psum[:, 2 * CH:4 * CH]
        layer0_stage(nc, S, dr)
        S.end_stage(nc)
        for st in STAGES[:upto]:
            st(nc, S, dr)
        with nc.semaphore("out_done") as out_done, nc.Block() as block:
            @block.sync
            def _(sp):
                sp.dma_start(natural(out), S.res[:, :, :]).then_inc(out_done, 16)
                sp.wait_ge(out_done, 16)


STAGES = [attention, mamba, moe]


def pack(inputs):
    a = {k: np.asarray(v) for k, v in inputs.items()}
    out = {"x": a["L0_attn_x"]}
    col = {"init_re": a["L0_attn_phazor_init_re"], "init_im": a["L0_attn_phazor_init_im"],
           "angle": a["L0_attn_phazor_angle"], "lnml": a["L0_attn_ln_minus_ln_phazor_abs"],
           "lc_re": a["L0_attn_last_conv_re"], "lc_im": a["L0_attn_last_conv_im"],
           "ln_scale": a["L0_attn_ln_phazor_scale"], "mu_r": a["L0_ffn_mu_r"], "mu_k": a["L0_ffn_mu_k"],
           "norm_g": a["L1_attn_norm_g"], "norm_b": a["L1_attn_norm_b"], "bq": a["L1_ffn_bq"], "bk": a["L1_ffn_bk"]}
    for n in ("ln1_g", "ln1_b", "ln2_g", "ln2_b"):
        col[n] = a[f"L1_ffn_{n}"]
    for d in "fb":
        for b in range(NB):
            rows = slice(P * b, P * (b + 1))
            for n in ("convb", "bdt", "D"):
                col[f"{d}_{n}{b}"] = a[f"L1_attn_{d}_{n}"][rows]
            for k in range(KC):
                col[f"{d}_convw{b}{k}"] = a[f"L1_attn_{d}_convw"][rows, 0, k]
            for s in range(NS):
                col[f"{d}_Alog{b}_{s}"] = a[f"L1_attn_{d}_Alog"][rows, s]
    out["b1"] = a["L1_ffn_b1"].reshape(NE, NFB, P).transpose(0, 2, 1)
    out["vecs"] = np.stack([col[n] for n in VECS], axis=1)
    out["w_mix"] = np.stack([a[f"L0_ffn_W_{n}"].T for n in "rkv"])
    for n in ("wq", "wk", "wv", "wo", "gate_w"):
        out[n] = a[f"L1_ffn_{n}"]
    for n in ("bv", "bo", "gate_b"):
        out[n] = np.broadcast_to(a[f"L1_ffn_{n}"][None, :], (P,) + a[f"L1_ffn_{n}"].shape)
    out["w1"], out["w2"], out["b2"] = a["L1_ffn_w1"], a["L1_ffn_w2"], a["L1_ffn_b2"]
    w_in, w_x, w_dt, w_out = [], [], [], []
    for d in "fb":
        w_in.append(a[f"L1_attn_{d}_Win"].T)
        wx = a[f"L1_attn_{d}_Wx"].T
        bc = wx[:, DR:]
        w_x.append(np.concatenate([bc, bc, bc, wx[:, :DR]], axis=1))
        w_dt.append(a[f"L1_attn_{d}_Wdt"].T)
        w_out.append(a[f"L1_attn_{d}_Wout"].T)
    out["w_in"], out["w_x"], out["w_dt"], out["w_out"] = (np.stack(w) for w in (w_in, w_x, w_dt, w_out))
    return {k: np.ascontiguousarray(v) for k, v in out.items()}


def kernel(**inputs):
    import concourse.bacc as bacc
    from concourse.bass_utils import run_bass_kernel_spmd

    nc = bacc.Bacc("TRN2", target_bir_lowering=False, num_devices=1)
    arrays = pack(inputs)
    dr = {k: nc.dram_tensor(f"in_{k}", v.shape, mybir.dt.from_np(v.dtype), kind="ExternalInput").ap()
          for k, v in arrays.items()}
    out = nc.dram_tensor("out_0", (1, T, P), F32, kind="ExternalOutput").ap()
    build(nc, dr, out)
    r = run_bass_kernel_spmd(nc, [{f"in_{k}": v for k, v in arrays.items()}], core_ids=[0])
    return r.results[0]["out_0"]
```

```python
from contextlib import ExitStack

import numpy as np

import concourse.bass as bass
from concourse import mybir

F32 = mybir.dt.float32
BF16 = mybir.dt.bfloat16
I32 = mybir.dt.int32
ALU = mybir.AluOpType
ACT = mybir.ActivationFunctionType
AX = mybir.AxisListType

P = 128
T = 2048
NT = T // P
CH = 512
NCH = T // CH
TPC = CH // P
EPS = 1e-5
TWO_PI = 2 * np.pi
SIN_SCALE = 6.283185
ROUND = 12582912.0

NH, HD = 16, 8
NE, NF = 8, 512
NFB = NF // P
DI, NS, KC, DR = 256, 16, 4, 8
NB = DI // P

VECS = ["init_re", "init_im", "angle", "lnml", "lc_re", "lc_im", "ln_scale", "mu_r", "mu_k",
        "norm_g", "norm_b", "ln1_g", "ln1_b", "ln2_g", "ln2_b", "bq", "bk"]
for _d in "fb":
    VECS += [f"{_d}_{n}{b}" for n in ("convb", "bdt", "D") for b in range(NB)]
    VECS += [f"{_d}_convw{b}{k}" for b in range(NB) for k in range(KC)]
    VECS += [f"{_d}_Alog{b}_{s}" for b in range(NB) for s in range(NS)]
VCOL = {n: i for i, n in enumerate(VECS)}
NV = len(VECS)


class Shared:

    def enter_sem(self, nc, name):
        handle = nc.alloc_semaphore(name=name)
        self.sems.append(handle)
        return handle

    def end_stage(self, nc):
        nc.clear_and_free_semaphores(self.sems)
        nc.all_engine_barrier()
        self.sems = []


def natural(dram):
    return dram.rearrange("o (i p) d -> p (o i) d", p=P)


def layer0_stage(nc, S, dr):
    with ExitStack() as ctx:
        def sb(name, shape, dt=F32):
            return ctx.enter_context(nc.sbuf_tensor(name, shape, dt))

        def sem(name):
            return S.enter_sem(nc, name)

        X = sb("l0_x", [P, NT, P])
        XN = sb("l0_xn", [P, NT, P])
        st6 = sb("l0_st6", [P, NT, 6])
        mv = sb("l0_mv", [P, NT, 2])
        rstd = sb("l0_rstd", [P, NT])
        lnv = sb("l0_lnv", [P, NT])
        rstd2 = sb("l0_rstd2", [P, NT])
        w2v = sb("l0_w2v", [P, NT])
        xpad = sb("l0_xpad", [P, T + 1])
        xT = xpad[:, 1:T + 1]
        x_prev = xpad[:, 0:T]
        ti = sb("l0_ti", [P, T], I32)
        turns = sb("l0_turns", [P, T])
        whole = sb("l0_whole", [P, T])
        sinT = sb("l0_sin", [P, T])
        cosT = sb("l0_cos", [P, T])
        p_re = sb("l0_pre", [P, T])
        p_im = sb("l0_pim", [P, T])
        s_mix = sb("l0_mix", [P, T])
        dx = sb("l0_dx", [P, T])
        xr = sb("l0_xr", [P, T])
        xk = sb("l0_xk", [P, T])
        sig = sb("l0_sig", [P, T])
        kact = sb("l0_kact", [P, T])
        W = sb("l0_w", [P, 3, P])
        sc = sb("l0_sc", [P, 16])
        (decay, dec_s, r_abs, gate, freq, a_re, a_im, na_im, l_re, l_im, tmp1, tmp2, in_re, in_im, tmp3,
         _) = [sc[:, i:i + 1] for i in range(16)]
        ident_w = S.ident

        banks = S.banks

        x_in = [sem(f"l0_x_in{q}") for q in range(4)]
        vec_in, w_in = sem("l0_vec_in"), sem("l0_w_in")
        pool_c, dve_c, act_c = sem("l0_pool_chain"), sem("l0_dve_chain"), sem("l0_act_chain")
        ident_ready = sem("l0_ident_ready")
        tok_ready = sem("l0_tok_ready")
        decay_ready, decs_ready, rabs_ready = sem("l0_decay"), sem("l0_decs"), sem("l0_rabs")
        turn_ready, trig_ready, turn_free = sem("l0_turn"), sem("l0_trig"), sem("l0_turn_free")
        var_ready, rstd_ready, xn_ready = sem("l0_var"), sem("l0_rstd_r"), sem("l0_xn_r")
        xT_psum, xT_ready = sem("l0_xT_psum"), sem("l0_xT_r")
        dx_ready, mixin_ready = sem("l0_dx_r"), sem("l0_mixin")
        proj_done, act_done, sq_done, val_done = sem("l0_proj"), sem("l0_actd"), sem("l0_sq"), sem("l0_val")
        mix_ready, back_done = sem("l0_mix_r"), sem("l0_back")
        var1_ready, rstd1_ready, w2_ready, rstd2_ready = sem("l0_v1"), sem("l0_r1"), sem("l0_w2"), sem("l0_r2")
        xh_ready, xh_psum, val_free = sem("l0_xh"), sem("l0_xhp"), sem("l0_vfree")
        block = ctx.enter_context(nc.Block())

        def V(name):
            return S.vec[:, VCOL[name]:VCOL[name] + 1]

        @block.sync
        def _(sp):
            sp.dma_start(S.vec[:, :], dr["vecs"]).then_inc(vec_in, 16)
            for q in range(4):
                sp.dma_start(X[:, 4 * q:4 * q + 4, :], natural(dr["x"])[:, 4 * q:4 * q + 4, :]).then_inc(x_in[q], 16)
            sp.dma_start(W[:, :, :], dr["w_mix"].rearrange("m c d -> c m d")).then_inc(w_in, 16)
            sp.wait_ge(w_in, 16)

        @block.gpsimd
        def _(pool):
            pool.iota(ti[:, :], pattern=[[1, T]], base=0, channel_multiplier=0).then_inc(tok_ready, 1)
            pool.memset(S.ident[:, :], 0.0).then_inc(pool_c, 1)
            pool.memset(S.flip[:, :], 0.0).then_inc(pool_c, 1)
            pool.memset(xpad[:, 0:1], 0.0).then_inc(pool_c, 1)
            pool.wait_ge(pool_c, 3)
            pool.affine_select(out=S.ident[:, :], in_=S.ident[:, :], compare_op=ALU.not_equal, fill=1.0,
                               base=0, pattern=[[-1, P]], channel_multiplier=1).then_inc(ident_ready, 1)
            pool.affine_select(out=S.flip[:, :], in_=S.flip[:, :], compare_op=ALU.not_equal, fill=1.0,
                               base=-(P - 1), pattern=[[1, P]], channel_multiplier=1).then_inc(ident_ready, 1)
            pool.wait_ge(xT_ready, NCH)
            pool.tensor_tensor(dx[:, :], xT, x_prev, ALU.subtract).then_inc(dx_ready, 1)
            for c in range(NCH):
                pool.wait_ge(act_done, 2 * c + 2)
                pool.tensor_tensor(kact[:, c * CH:(c + 1) * CH], kact[:, c * CH:(c + 1) * CH],
                                   kact[:, c * CH:(c + 1) * CH], ALU.mult).then_inc(sq_done, 1)

        @block.scalar
        def _(act):
            act.wait_ge(vec_in, 16)
            act.activation(decay, V("lnml"), ACT.Exp).then_inc(decay_ready, 1)
            act.wait_ge(decs_ready, 1)
            act.activation(r_abs, dec_s, ACT.Exp, scale=-1.0).then_inc(rabs_ready, 1)
            act.wait_ge(var_ready, 1)
            act.activation(lnv[:, :], w2v[:, :], ACT.Ln).then_inc(act_c, 1)
            act.wait_ge(act_c, 1)
            act.activation(rstd[:, :], lnv[:, :], ACT.Exp, scale=-0.5).then_inc(rstd_ready, 1)
            for c in range(NCH):
                act.wait_ge(xT_psum, c + 1)
                act.activation(xpad[:, 1 + c * CH:1 + (c + 1) * CH], banks[c][:, :], ACT.Copy).then_inc(xT_ready, 1)
            act.wait_ge(turn_ready, 1)
            act.activation(sinT[:, :], turns[:, :], ACT.Sin, scale=SIN_SCALE).then_inc(trig_ready, 1)
            act.wait_ge(turn_ready, 2)
            act.activation(cosT[:, :], whole[:, :], ACT.Sin, scale=SIN_SCALE).then_inc(trig_ready, 1)
            for c in range(NCH):
                act.wait_ge(proj_done, 2 * c + 1)
                act.activation(sig[:, c * CH:(c + 1) * CH], banks[2 * (c % 2)][:, :], ACT.Sigmoid).then_inc(act_done, 1)
                act.wait_ge(proj_done, 2 * c + 2)
                act.activation(kact[:, c * CH:(c + 1) * CH], banks[2 * (c % 2) + 1][:, :], ACT.Relu).then_inc(act_done, 1)
            act.wait_ge(var1_ready, 1)
            act.activation(lnv[:, :], w2v[:, :], ACT.Ln).then_inc(act_c, 1)
            act.wait_ge(act_c, 2)
            act.activation(rstd[:, :], lnv[:, :], ACT.Exp, scale=-0.5).then_inc(rstd1_ready, 1)
            act.wait_ge(w2_ready, 1)
            act.activation(lnv[:, :], w2v[:, :], ACT.Ln).then_inc(act_c, 1)
            act.wait_ge(act_c, 3)
            act.activation(rstd2[:, :], lnv[:, :], ACT.Exp, scale=-0.5).then_inc(rstd2_ready, 1)
            for c in range(NCH):
                act.wait_ge(xh_psum, 2 * c + 1)
                act.activation(S.xh[:, 0, c * CH:(c + 1) * CH], banks[c][:, :], ACT.Copy).then_inc(act_c, 1)
                act.wait_ge(xh_psum, 2 * c + 2)
                act.activation(S.xh[:, 1, T - (c + 1) * CH:T - c * CH], banks[4 + c][:, :], ACT.Copy).then_inc(act_c, 1)

        @block.vector
        def _(dve):
            count = [0]

            def link(ins):
                count[0] += 1
                ins.then_inc(dve_c, 1)
                dve.wait_ge(dve_c, count[0])

            dve.wait_ge(vec_in, 16)
            dve.wait_ge(decay_ready, 1)
            dve.tensor_tensor(dec_s, decay, V("ln_scale"), ALU.mult).then_inc(decs_ready, 1)
            link(dve.tensor_scalar(freq, V("angle"), V("ln_scale"), 1.0 / TWO_PI, ALU.mult, ALU.mult))
            for q in range(4):
                dve.wait_ge(x_in[q], 16)
                for i in range(4 * q, 4 * q + 4):
                    last = dve.bn_stats(st6[:, i, :], X[:, i, :])
            link(last)
            for i in range(NT):
                last = dve.bn_aggr(mv[:, i, :], st6[:, i, :])
            link(last)
            dve.tensor_scalar(w2v[:, :], mv[:, :, 1], EPS, None, ALU.add).then_inc(var_ready, 1)
            dve.wait_ge(rstd_ready, 1)
            for i in range(NT):
                dve.tensor_scalar(XN[:, i, :], X[:, i, :], mv[:, i, 0:1], rstd[:, i:i + 1],
                                  ALU.subtract, ALU.mult).then_inc(xn_ready, 1)
            dve.wait_ge(tok_ready, 1)
            link(dve.tensor_copy(sinT[:, :], ti[:, :]))
            link(dve.tensor_scalar(turns[:, :], sinT[:, :], freq, None, ALU.mult))
            link(dve.tensor_scalar(whole[:, :], turns[:, :], ROUND, -ROUND, ALU.add, ALU.add))
            link(dve.tensor_tensor(turns[:, :], turns[:, :], whole[:, :], ALU.subtract))
            link(dve.tensor_scalar(p_re[:, :], turns[:, :], 0.25, None, ALU.add))
            link(dve.tensor_scalar(p_im[:, :], p_re[:, :], ROUND, -ROUND, ALU.add, ALU.add))
            dve.sem_inc(turn_ready, 1)
            link(dve.tensor_tensor(whole[:, :], p_re[:, :], p_im[:, :], ALU.subtract))
            dve.sem_inc(turn_ready, 1)
            dve.wait_ge(rabs_ready, 1)
            link(dve.tensor_scalar(gate, r_abs, -1.0, 1.0, ALU.mult, ALU.add))
            dve.tensor_tensor(a_re, V("init_re"), gate, ALU.mult)
            dve.tensor_tensor(l_re, V("lc_re"), gate, ALU.mult)
            dve.tensor_tensor(l_im, V("lc_im"), gate, ALU.mult)
            link(dve.tensor_tensor(a_im, V("init_im"), gate, ALU.mult))
            link(dve.tensor_scalar(na_im, a_im, -1.0, None, ALU.mult))
            dve.wait_ge(trig_ready, 2)
            dve.tensor_tensor(tmp1, l_re, cosT[:, 1:2], ALU.mult)
            dve.tensor_tensor(tmp2, l_im, sinT[:, 1:2], ALU.mult)
            link(dve.tensor_tensor(tmp3, l_re, sinT[:, 1:2], ALU.mult))
            dve.tensor_tensor(in_re, tmp1, tmp2, ALU.subtract)
            link(dve.scalar_tensor_tensor(out=in_im, in0=l_im, scalar=cosT[:, 1:2], in1=tmp3,
                                          op0=ALU.mult, op1=ALU.add))
            dve.tensor_scalar(p_re[:, :], cosT[:, :], a_re, None, ALU.mult)
            link(dve.tensor_scalar(p_im[:, :], cosT[:, :], a_im, None, ALU.mult))
            dve.scalar_tensor_tensor(out=p_re[:, :], in0=sinT[:, :], scalar=a_im, in1=p_re[:, :],
                                     op0=ALU.mult, op1=ALU.add)
            dve.wait_ge(xT_ready, NCH)
            link(dve.tensor_scalar(tmp1, a_re, -1.0, None, ALU.mult))
            link(dve.scalar_tensor_tensor(out=p_im[:, :], in0=sinT[:, :], scalar=tmp1, in1=p_im[:, :],
                                          op0=ALU.mult, op1=ALU.add))
            dve.tensor_tensor(p_re[:, :], p_re[:, :], xT, ALU.mult)
            link(dve.tensor_tensor(p_im[:, :], p_im[:, :], xT, ALU.mult))
            dve.wait_ge(dx_ready, 1)
            dve.scalar_tensor_tensor(out=xr[:, :], in0=dx[:, :], scalar=V("mu_r"), in1=x_prev,
                                     op0=ALU.mult, op1=ALU.add).then_inc(mixin_ready, 1)
            dve.scalar_tensor_tensor(out=xk[:, :], in0=dx[:, :], scalar=V("mu_k"), in1=x_prev,
                                     op0=ALU.mult, op1=ALU.add).then_inc(mixin_ready, 1)
            dve.tensor_tensor_scan(turns[:, :], r_abs.to_broadcast([P, T]), p_re[:, :], in_re, ALU.mult, ALU.add)
            link(dve.tensor_tensor_scan(whole[:, :], r_abs.to_broadcast([P, T]), p_im[:, :], in_im,
                                        ALU.mult, ALU.add))
            dve.tensor_tensor(p_re[:, :], turns[:, :], cosT[:, :], ALU.mult)
            link(dve.tensor_tensor(p_im[:, :], whole[:, :], sinT[:, :], ALU.mult))
            link(dve.tensor_tensor(s_mix[:, :], p_re[:, :], p_im[:, :], ALU.subtract))
            for c in range(NCH):
                sl = slice(c * CH, (c + 1) * CH)
                dve.wait_ge(val_done, c + 1)
                dve.wait_ge(act_done, 2 * c + 1)
                dve.tensor_tensor(xr[:, sl], banks[4 + c % 2][:, :], sig[:, sl], ALU.mult).then_inc(val_free, 1)
                dve.wait_ge(val_free, c + 1)
                dve.tensor_tensor(s_mix[:, sl], s_mix[:, sl], xr[:, sl], ALU.add).then_inc(mix_ready, 1)
            for c in range(NCH):
                dve.wait_ge(back_done, c + 1)
                link(dve.tensor_tensor(X[:, TPC * c:TPC * (c + 1), :], X[:, TPC * c:TPC * (c + 1), :],
                                       banks[c][:, :].rearrange("p (i d) -> p i d", d=P), ALU.add))
                for i in range(TPC * c, TPC * (c + 1)):
                    last = dve.bn_stats(st6[:, i, :], X[:, i, :])
            link(last)
            for i in range(NT):
                last = dve.bn_aggr(mv[:, i, :], st6[:, i, :])
            link(last)
            dve.tensor_scalar(w2v[:, :], mv[:, :, 1], EPS, None, ALU.add).then_inc(var1_ready, 1)
            dve.wait_ge(rstd1_ready, 1)
            for i in range(NT):
                last = dve.tensor_scalar(S.xn1[:, i, :], X[:, i, :], mv[:, i, 0:1], rstd[:, i:i + 1],
                                         ALU.subtract, ALU.mult)
            link(dve.tensor_tensor(w2v[:, :], rstd[:, :], rstd[:, :], ALU.mult))
            link(dve.tensor_tensor(w2v[:, :], w2v[:, :], mv[:, :, 1], ALU.mult))
            link(dve.tensor_scalar(w2v[:, :], w2v[:, :], EPS, None, ALU.add))
            dve.sem_inc(w2_ready, 1)
            link(dve.tensor_tensor(S.res[:, :, :], X[:, :, :], S.xn1[:, :, :], ALU.add))
            dve.wait_ge(rstd2_ready, 1)
            for i in range(NT):
                dve.tensor_scalar(XN[:, i, :], S.xn1[:, i, :], rstd2[:, i:i + 1], None, ALU.mult).then_inc(xh_ready, 1)

        @block.tensor
        def _(pe):
            pe.wait_ge(ident_ready, 2)
            for i in range(NT):
                pe.wait_ge(xn_ready, i + 1)
                mm = pe.transpose(banks[i // TPC][:, P * (i % TPC):P * (i % TPC + 1)], XN[:, i, :], ident_w[:, :])
                if i % TPC == TPC - 1:
                    mm.then_inc(xT_psum, 1)
            pe.wait_ge(w_in, 16)
            pe.wait_ge(mixin_ready, 2)
            pe.wait_ge(xT_ready, NCH)

            def value(c):
                pe.wait_ge(sq_done, c + 1)
                if c >= 2:
                    pe.wait_ge(val_free, c - 1)
                pe.matmul(banks[4 + c % 2][:, :], W[:, 2, :], kact[:, c * CH:(c + 1) * CH],
                          start=True, stop=True).then_inc(val_done, 1)

            for c in range(NCH):
                if c >= 2:
                    pe.wait_ge(act_done, 2 * (c - 1))
                pe.matmul(banks[2 * (c % 2)][:, :], W[:, 0, :], xr[:, c * CH:(c + 1) * CH],
                          start=True, stop=True).then_inc(proj_done, 1)
                pe.matmul(banks[2 * (c % 2) + 1][:, :], W[:, 1, :], xk[:, c * CH:(c + 1) * CH],
                          start=True, stop=True).then_inc(proj_done, 1)
                if c >= 1:
                    value(c - 1)
            value(NCH - 1)
            pe.wait_ge(act_done, 2 * NCH)
            for c in range(NCH):
                pe.wait_ge(mix_ready, c + 1)
                for i in range(TPC * c, TPC * (c + 1)):
                    mm = pe.transpose(banks[c][:, P * (i % TPC):P * (i % TPC + 1)],
                                      s_mix[:, P * i:P * (i + 1)], ident_w[:, :])
                mm.then_inc(back_done, 1)
            pe.wait_ge(w2_ready, 1)
            for c in range(NCH):
                pe.wait_ge(xh_ready, TPC * (c + 1))
                for i in range(TPC):
                    mm = pe.transpose(banks[c][:, P * i:P * (i + 1)], XN[:, TPC * c + i, :], ident_w[:, :])
                mm.then_inc(xh_psum, 1)
                for i in range(TPC):
                    k = TPC - 1 - i
                    mm = pe.matmul(banks[4 + c][:, P * k:P * (k + 1)], XN[:, TPC * c + i, :], S.flip[:, :],
                                   start=True, stop=True)
                mm.then_inc(xh_psum, 1)



NG = 4
HG = NH // NG
DQ = 9 * HD
DM = DQ + 3
VW = 32


def attention_prep_stage(nc, S, dr):
    with ExitStack() as ctx:
        def sb(name, shape, dt=F32):
            return ctx.enter_context(nc.sbuf_tensor(name, shape, dt))

        def sem(name):
            return S.enter_sem(nc, name)

        W = sb("ap_w", [P, 3, P])
        bv = sb("ap_bv", [P, P])
        hn = sb("ap_hn", [P, T])
        rem = sb("ap_rem", [P, T])
        parts = sb("ap_parts", [P, 3, T], BF16)
        banks = S.banks
        w_in, dve_c = sem("ap_w_in"), sem("ap_dve_chain")
        ones_ready, ones_in = sem("ap_ones_ready"), sem("ap_ones_in")
        hn_ready, qk_psum, v_psum = sem("ap_hn"), sem("ap_qk_psum"), sem("ap_v_psum")
        f_ready, hi_ready, v_ready = sem("ap_f"), sem("ap_hi"), sem("ap_v")
        rem1_ready, parts_ready = sem("ap_rem1"), sem("ap_parts_ready")
        stored = [sem("ap_stored_q"), sem("ap_stored_k")]
        block = ctx.enter_context(nc.Block())

        def V(name):
            return S.vec[:, VCOL[name]:VCOL[name] + 1]

        @block.sync
        def _(sp):
            for i, n in enumerate(("wq", "wk", "wv")):
                sp.dma_start(W[:, i, :], dr[n]).then_inc(w_in, 16)
            sp.dma_start(bv[:, :], dr["bv"]).then_inc(w_in, 16)
            sp.wait_ge(ones_ready, 1)
            for g in range(NG):
                sp.dma_start(S.ks[DQ:DM, HG * g * T:HG * (g + 1) * T].rearrange("r (h t) -> r h t", t=T),
                             S.ones[0:3, :].unsqueeze(1).to_broadcast([3, HG, T])).then_inc(ones_in, 16)
            for w in range(2):
                sp.wait_ge(parts_ready, w + 1)
                sp.dma_start(S.qk_dram[w].rearrange("i f t -> f i t"), parts[:, :, :]).then_inc(stored[w], 16)
                sp.wait_ge(stored[w], 16)
            sp.wait_ge(ones_in, 16 * NG)

        @block.gpsimd
        def _(pool):
            pool.memset(S.ones[:, :], 1.0).then_inc(ones_ready, 1)

        @block.scalar
        def _(act):
            for w, bias in enumerate(("bq", "bk")):
                if w:
                    act.wait_ge(parts_ready, w)
                    act.wait_ge(stored[0], 16)
                for c in range(NCH):
                    act.wait_ge(qk_psum, NCH * w + c + 1)
                    act.activation(rem[:, c * CH:(c + 1) * CH], banks[4 * w + c][:, :], ACT.Identity,
                                   bias=V(bias)).then_inc(f_ready, 1)
                act.wait_ge(f_ready, NCH * (w + 1))
                act.activation(parts[:, 0, :], rem[:, :], ACT.Copy).then_inc(hi_ready, 1)

        @block.vector
        def _(dve):
            count = [0]

            def link(ins):
                count[0] += 1
                ins.then_inc(dve_c, 1)
                dve.wait_ge(dve_c, count[0])

            link(dve.tensor_copy(S.identb[:, :], S.ident[:, :]))
            dve.tensor_scalar(hn[:, :], S.xh[:, 0, :], V("ln1_g"), V("ln1_b"), ALU.mult, ALU.add).then_inc(hn_ready, 1)
            for w in range(2):
                dve.wait_ge(hi_ready, w + 1)
                link(dve.tensor_tensor(rem[:, :], rem[:, :], parts[:, 0, :], ALU.subtract))
                link(dve.tensor_copy(parts[:, 1, :], rem[:, :]))
                dve.tensor_tensor(parts[:, 2, :], rem[:, :], parts[:, 1, :], ALU.subtract).then_inc(parts_ready, 1)
            dve.wait_ge(w_in, 64)
            for c in range(NCH):
                dve.wait_ge(v_psum, c + 1)
                for i in range(TPC):
                    dve.tensor_tensor(S.v[:, :, TPC * c + i, :],
                                      banks[c][:, P * i:P * (i + 1)].rearrange("p (g d) -> p g d", g=NG),
                                      bv[:, :].rearrange("p (g d) -> p g d", g=NG), ALU.add).then_inc(v_ready, 1)

        @block.tensor
        def _(pe):
            pe.wait_ge(w_in, 64)
            pe.wait_ge(hn_ready, 1)
            for w in range(2):
                for c in range(NCH):
                    pe.matmul(banks[4 * w + c][:, :], W[:, w, :], hn[:, c * CH:(c + 1) * CH],
                              start=True, stop=True).then_inc(qk_psum, 1)
            pe.wait_ge(f_ready, NCH)
            for c in range(NCH):
                for i in range(TPC):
                    t = TPC * c + i
                    mm = pe.matmul(banks[c][:, P * i:P * (i + 1)], hn[:, P * t:P * (t + 1)], W[:, 2, :],
                                   start=True, stop=True)
                mm.then_inc(v_psum, 1)


def attention_stage(nc, S, dr):
    with ExitStack() as ctx:
        def sb(name, shape, dt=F32):
            return ctx.enter_context(nc.sbuf_tensor(name, shape, dt))

        def sem(name):
            return S.enter_sem(nc, name)

        vg = sb("at_vg", [P, NT, HG, VW])
        probs = sb("at_probs", [P, 2, 2, 2 * CH])
        osb = sb("at_osb", [P, CH])
        ROWS = HG * TPC
        NMAX = ROWS * NCH
        PER = NMAX // NT
        LEAD = 8 * PER
        TURN = (NMAX - LEAD) // PER
        mpart = sb("at_mpart", [P, ROWS, NCH])
        mx = sb("at_mx", [P, HG, TPC])
        mrem = sb("at_mrem", [P, HG, TPC])
        m3 = sb("at_m3", [P, HG, 3, TPC], BF16)
        mrow = sb("at_mrow", [3 * ROWS, P], BF16)
        rden = sb("at_rden", [P, TPC, HG])
        s_banks = [[S.banks[0], S.banks[1]], [S.banks[2], S.banks[3]]]
        s_pair = S.sc01, S.sc23
        o_bank, t_bank, m_bank = S.banks[4], S.banks[5], [S.banks[6], S.banks[7]]
        t_bf = t_bank.bitcast(BF16)

        q_in = [sem(f"at_q_in{g}") for g in range(NG)]
        k_in = [sem(f"at_k_in{g}") for g in range(NG)]
        mrow_in = sem("at_mrow_in")
        dve_c, pool_c, sp_c, pe_c = (sem(f"at_{n}_chain") for n in ("dve", "pool", "sp", "pe"))
        max_scores, max_free = sem("at_max_scores"), sem("at_max_free")
        m3_ready, mT_psum, mrow_ready = sem("at_m3"), sem("at_mT"), sem("at_mrow_ready")
        scores = sem("at_scores")
        probs_ready, probs_free = sem("at_probs_ready"), sem("at_probs_free")
        vg_ready = sem("at_vg_ready")
        o_copied, o_turned, o_normed = sem("at_o_copied"), sem("at_o_turned"), sem("at_o_normed")
        block = ctx.enter_context(nc.Block())
        HT = HG * T
        NSTEP = NG * NCH

        assert NCH == 4

        def group_of(s):
            return (s >> 2) & 3

        def chunk_of(s):
            return s & 3

        @block.sync
        def _(sp):
            def load(g):
                for h in range(HG * g, HG * (g + 1)):
                    for i in range(3):
                        rows = slice(3 * HD * i, 3 * HD * (i + 1))
                        sp.dma_start(S.qs[rows, h * T:(h + 1) * T],
                                     S.qk_dram[0][i:i + 1, HD * h:HD * (h + 1), :].to_broadcast([3, HD, T]))\
                            .then_inc(q_in[g], 16)
                        sp.dma_start(S.ks[rows, h * T:(h + 1) * T],
                                     S.qk_dram[1][:, HD * h:HD * (h + 1), :]).then_inc(k_in[g], 16)

            def place_max(s):
                sp.wait_ge(mrow_ready, s + 1)
                sp.sem_inc(sp_c, 1)
                for j in range(HG):
                    sp.dma_start(S.qs[DQ:DM, bass.ds(group_of(s) * HT + chunk_of(s) * CH + j * T, CH)]
                                 .rearrange("r (i p) -> r i p", p=P),
                                 mrow[3 * TPC * j:3 * TPC * (j + 1), :]).then_inc(mrow_in, 16)

            load(0)
            place_max(0)
            for g in range(1, NG):
                load(g)
            with sp.Fori(1, NSTEP) as s:
                place_max(s)
            sp.wait_ge(mrow_in, 16 * HG * NSTEP)

        @block.gpsimd
        def _(pool):
            pool.memset(vg[:, :, :, :], 0.0).then_inc(pool_c, 1)
            pool.wait_ge(pool_c, 1)
            pool.memset(vg[:, :, :, HD:HD + 1], 1.0).then_inc(pool_c, 1)
            pool.wait_ge(pool_c, 2)
            with pool.Fori(0, NG) as g:
                pool.wait_ge(probs_free, g * (NCH * NT) + 2)
                pool.sem_inc(pool_c, 1)
                pool.tensor_copy(vg[:, :, :, 0:HD],
                                 S.v[:, bass.ds(g, 1), :, :].rearrange("p o i (j d) -> p (o i) j d", d=HD))\
                    .then_inc(vg_ready, 1)

        @block.scalar
        def _(act):
            with act.Fori(0, NSTEP) as s:
                for kt in range(NT):
                    act.wait_ge(probs_free, s * NT + (kt + 1))
                    for p in range(2):
                        act.wait_ge(scores, s * (2 * NT) + (2 * kt + p + 1))
                        act.activation(probs[:, kt % 2, p, :], s_pair[p], ACT.Exp,
                                       scale=float(HD) ** -0.5).then_inc(probs_ready, 1)

        @block.vector
        def _(dve):
            def maxima(s, lo, hi):
                for m in range(lo, min(hi, NMAX)):
                    row, kc = divmod(m, NCH)
                    dve.wait_ge(max_scores, s * NMAX + (m + 1))
                    dve.reduce_max(mpart[:, row, kc:kc + 1], m_bank[m % 2], AX.X).then_inc(max_free, 1)

            def split_max(s):
                dve.wait_ge(max_free, s * NMAX + (NMAX + 2))
                dve.tensor_reduce(mx[:, :, :].rearrange("p j i -> p (j i)"), mpart[:, :, :], AX.X, ALU.max).then_inc(dve_c, 1)
                dve.wait_ge(dve_c, s * 6 + 1)
                dve.tensor_scalar(mrem[:, :, :], mx[:, :, :], -1.0, None, ALU.mult).then_inc(dve_c, 1)
                dve.wait_ge(dve_c, s * 6 + 2)
                dve.tensor_copy(m3[:, :, 0, :], mrem[:, :, :]).then_inc(dve_c, 1)
                dve.wait_ge(dve_c, s * 6 + 3)
                dve.tensor_tensor(mrem[:, :, :], mrem[:, :, :], m3[:, :, 0, :], ALU.subtract).then_inc(dve_c, 1)
                dve.wait_ge(dve_c, s * 6 + 4)
                dve.tensor_copy(m3[:, :, 1, :], mrem[:, :, :]).then_inc(dve_c, 1)
                dve.wait_ge(dve_c, s * 6 + 5)
                dve.tensor_tensor(m3[:, :, 2, :], mrem[:, :, :], m3[:, :, 1, :], ALU.subtract).then_inc(dve_c, 1)
                dve.wait_ge(dve_c, s * 6 + 6)
                dve.sem_inc(m3_ready, 1)

            def place_rows(s, first=False):
                if not first:
                    dve.wait_ge(mrow_in, s * (16 * HG))
                dve.wait_ge(mT_psum, s + 1)
                dve.tensor_copy(mrow[:, :], t_bf[0:3 * ROWS, 0:P]).then_inc(mrow_ready, 1)

            def take_out(s):
                dve.wait_ge(probs_free, s * NT + (NT + 2))
                dve.tensor_copy(osb[:, :], o_bank).then_inc(o_copied, 1)

            def norm_out(s):
                dve.wait_ge(o_turned, s + 1)
                turned = t_bank.rearrange("p (i j c) -> p i j c", i=TPC, c=VW)
                dve.reciprocal(rden[:, :, :], turned[:, :, :, HD]).then_inc(o_normed, 1)
                dve.wait_ge(o_normed, s * 2 + 3)
                width = TPC * HG * HD
                dve.tensor_tensor(S.v.rearrange("p g i c -> p (g i c)")[:, bass.ds(s * width, width)]
                                  .rearrange("p (i j d) -> p i j d", i=TPC, d=HD),
                                  turned[:, :, :, 0:HD], rden[:, :, :].unsqueeze(3).to_broadcast([P, TPC, HG, HD]),
                                  ALU.mult).then_inc(o_normed, 1)
                dve.wait_ge(o_normed, s * 2 + 4)

            def step(s, first=False, ahead=2):
                for kt in range(NT):
                    if not first and kt == 1:
                        take_out(s - 1)
                    if ahead >= 1 and kt == TURN:
                        split_max(s + 1)
                    if ahead >= 1 and kt == TURN + 2:
                        place_rows(s + 1)
                    if ahead >= 1 and kt < TURN:
                        maxima(s + 1, LEAD + PER * kt, LEAD + PER * (kt + 1))
                    if ahead >= 2 and kt >= TURN:
                        maxima(s + 2, PER * (kt - TURN), PER * (kt - TURN + 1))
                    if not first and kt == 3:
                        norm_out(s - 1)

            dve.sem_inc(max_free, 2)
            dve.sem_inc(o_copied, 1)
            dve.sem_inc(o_normed, 2)
            maxima(0, 0, NMAX)
            split_max(0)
            maxima(1, 0, PER)
            place_rows(0, first=True)
            maxima(1, PER, LEAD)
            step(0, first=True)
            with dve.Fori(1, NSTEP - 2) as s:
                step(s)
            step(NSTEP - 2, ahead=1)
            step(NSTEP - 1, ahead=0)
            take_out(NSTEP - 1)
            norm_out(NSTEP - 1)

        @block.tensor
        def _(pe):
            def maxima(s, lo, hi):
                heads, queries = group_of(s) * HT, group_of(s) * HT + chunk_of(s) * CH
                for m in range(lo, min(hi, NMAX)):
                    row, kc = divmod(m, NCH)
                    j, i = divmod(row, TPC)
                    pe.wait_ge(max_free, s * NMAX + (m + 1))
                    pe.matmul(m_bank[m % 2], S.qs[0:DQ, bass.ds(queries + (j * T + i * P), P)],
                              S.ks[0:DQ, bass.ds(heads + (j * T + kc * CH), CH)], start=True, stop=True)\
                        .then_inc(max_scores, 1)

            def turn_max(n):
                pe.wait_ge(m3_ready, n)
                pe.sem_inc(pe_c, 1)
                pe.transpose(t_bf[0:3 * ROWS, 0:P], m3[:, :, :, :].rearrange("p j r i -> p (j r i)"),
                             S.identb[:, :]).then_inc(mT_psum, 1)

            def score(s, kt, p, b):
                heads, queries = group_of(s) * HT, group_of(s) * HT + chunk_of(s) * CH
                if b == 0:
                    pe.wait_ge(probs_ready, s * (2 * NT) + (2 * kt + p + 1))
                j = 2 * p + b
                mm = pe.matmul(s_banks[p][b], S.ks[0:DM, bass.ds(heads + (j * T + kt * P), P)],
                               S.qs[0:DM, bass.ds(queries + j * T, CH)], start=True, stop=True)
                if b:
                    mm.then_inc(scores, 1)

            def weigh(s, kt):
                if kt == 0:
                    pe.wait_ge(o_copied, s + 1)
                pe.wait_ge(probs_ready, s * (2 * NT) + (2 * kt + 4))
                for j in range(HG):
                    mm = pe.matmul(o_bank[VW * j:VW * (j + 1), :], vg[:, kt, j, :],
                                   probs[:, kt % 2, j // 2, CH * (j % 2):CH * (j % 2 + 1)],
                                   start=(kt == 0), stop=(kt == NT - 1), tile_position=(0, VW * j))
                mm.then_inc(probs_free, 1)

            def turn_out(s):
                pe.wait_ge(mrow_ready, s + 1)
                pe.wait_ge(o_copied, s + 2)
                for i in range(TPC):
                    mm = pe.transpose(t_bank[:, P * i:P * (i + 1)], osb[:, P * i:P * (i + 1)], S.ident[:, :])
                mm.then_inc(o_turned, 1)

            def step(s, first=False, ahead=2):
                pe.wait_ge(mrow_in, s * (16 * HG) + 16 * HG)

                def beside(kt, lo, hi):
                    if ahead >= 1 and kt < TURN:
                        maxima(s + 1, LEAD + PER * kt + lo, LEAD + PER * kt + hi)
                    if ahead >= 2 and kt >= TURN:
                        maxima(s + 2, PER * (kt - TURN) + lo, PER * (kt - TURN) + hi)

                for kt in range(NT):
                    score(s, kt, 0, 0)
                    score(s, kt, 0, 1)
                    beside(kt, 0, 1)
                    score(s, kt, 1, 0)
                    score(s, kt, 1, 1)
                    beside(kt, 1, 2)
                    if kt:
                        if kt == 1:
                            pe.wait_ge(vg_ready, group_of(s) + 1)
                        weigh(s, kt - 1)
                    elif not first:
                        weigh(s - 1, NT - 1)
                    beside(kt, 2, 3)
                    beside(kt, 3, 4)
                    if not first and kt == 2:
                        turn_out(s - 1)
                    if ahead >= 1 and kt == TURN + 1:
                        pe.wait_ge(o_normed, s * 2 + 2)
                        turn_max(s + 2)

            pe.sem_inc(probs_free, 2)
            pe.sem_inc(probs_ready, 2)
            pe.wait_ge(q_in[0], 16 * 3 * HG)
            pe.wait_ge(k_in[0], 16 * 3 * HG)
            maxima(0, 0, NMAX)
            maxima(1, 0, PER)
            turn_max(1)
            maxima(1, PER, LEAD)
            step(0, first=True)
            for n in range(1, NG):
                pe.wait_ge(q_in[n], 16 * 3 * HG)
                pe.wait_ge(k_in[n], 16 * 3 * HG)
            with pe.Fori(1, NSTEP - 2) as s:
                step(s)
            step(NSTEP - 2, ahead=1)
            step(NSTEP - 1, ahead=0)
            weigh(NSTEP - 1, NT - 1)
            turn_out(NSTEP - 1)


def attention_out_stage(nc, S, dr):
    with ExitStack() as ctx:
        def sb(name, shape, dt=F32):
            return ctx.enter_context(nc.sbuf_tensor(name, shape, dt))

        def sem(name):
            return S.enter_sem(nc, name)

        W = sb("ao_w", [P, P])
        bo = sb("ao_bo", [P, P])
        oT = sb("ao_oT", [P, T])
        nat = sb("ao_nat", [P, NT, P])
        w_in, oT_psum, oT_ready, proj_done, dve_c = (sem("ao_w_in"), sem("ao_oT_psum"), sem("ao_oT_ready"),
                                                     sem("ao_proj"), sem("ao_dve_chain"))
        nat_ready = sem("ao_nat_ready")
        banks = S.banks
        block = ctx.enter_context(nc.Block())

        @block.sync
        def _(sp):
            sp.dma_start(W[:, :], dr["wo"]).then_inc(w_in, 16)
            sp.dma_start(bo[:, :], dr["bo"]).then_inc(w_in, 16)
            sp.wait_ge(w_in, 32)

        @block.scalar
        def _(act):
            for c in range(NCH):
                act.wait_ge(oT_psum, c + 1)
                act.activation(oT[:, c * CH:(c + 1) * CH], banks[c][:, :], ACT.Copy).then_inc(oT_ready, 1)

        @block.tensor
        def _(pe):
            for c in range(NCH):
                pe.wait_ge(nat_ready, c + 1)
                for i in range(TPC):
                    mm = pe.transpose(banks[c][:, P * i:P * (i + 1)], nat[:, TPC * c + i, :], S.ident[:, :])
                mm.then_inc(oT_psum, 1)
            pe.wait_ge(w_in, 32)
            for c in range(NCH):
                pe.wait_ge(oT_ready, c + 1)
                for i in range(TPC):
                    t = TPC * c + i
                    mm = pe.matmul(banks[4 + c][:, P * i:P * (i + 1)], oT[:, P * t:P * (t + 1)], W[:, :],
                                   start=True, stop=True)
                mm.then_inc(proj_done, 1)

        @block.vector
        def _(dve):
            for c in range(NCH):
                tiles = slice(TPC * c, TPC * (c + 1))
                dve.tensor_copy(nat[:, tiles, :].rearrange("p i (g d) -> p g i d", g=NG),
                                S.v[:, :, tiles, :]).then_inc(nat_ready, 1)
            dve.wait_ge(w_in, 32)
            for c in range(NCH):
                x2 = S.xn1[:, TPC * c:TPC * (c + 1), :]
                r = S.res[:, TPC * c:TPC * (c + 1), :]
                dve.wait_ge(proj_done, c + 1)
                dve.tensor_tensor(x2, x2, banks[4 + c][:, :].rearrange("p (i d) -> p i d", d=P), ALU.add).then_inc(dve_c, 1)
                dve.wait_ge(dve_c, 3 * c + 1)
                dve.tensor_tensor(x2, x2, bo[:, :].unsqueeze(1).to_broadcast([P, TPC, P]), ALU.add).then_inc(dve_c, 1)
                dve.wait_ge(dve_c, 3 * c + 2)
                dve.tensor_tensor(r, r, x2, ALU.add).then_inc(dve_c, 1)


def attention(nc, S, dr):
    with ExitStack() as ctx:
        S.qk_dram = [nc.dram_tensor(f"{n}_parts", [3, P, T], BF16).ap() for n in "qk"]
        S.v = ctx.enter_context(nc.sbuf_tensor("at_v", [P, NG, NT, HG * HD], F32))[:, :, :, :]
        S.identb = ctx.enter_context(nc.sbuf_tensor("identb", [P, P], BF16))
        with ExitStack() as big:
            S.qs = big.enter_context(nc.sbuf_tensor("at_qs", [P, NH * T], BF16))
            S.ks = big.enter_context(nc.sbuf_tensor("at_ks", [P, NH * T], BF16))
            with ExitStack() as c2:
                S.ones = c2.enter_context(nc.sbuf_tensor("at_ones", [3, T], BF16))
                attention_prep_stage(nc, S, dr)
                S.end_stage(nc)
            attention_stage(nc, S, dr)
            S.end_stage(nc)
        attention_out_stage(nc, S, dr)
        S.end_stage(nc)


BC = 2 * NS
BC3 = 3 * BC


def mamba_prep_stage(nc, S, dr, d):
    name = "fb"[d]
    with ExitStack() as ctx:
        def sb(n, shape, dt=F32):
            return ctx.enter_context(nc.sbuf_tensor(f"mp{name}_{n}", shape, dt))

        def sem(n):
            return S.enter_sem(nc, f"mp{name}_{n}")

        w_in_sb = sb("w_in", [P, 2 * DI])
        w_x = sb("w_x", [P, NB, BC3 + DR])
        w_dt = sb("w_dt", [P, DI])
        xm = sb("xm", [P, T])
        up = sb("up", [P, NB, T + KC - 1])
        rem = xm
        soft = up
        mid = sb("mid", [P, T], BF16)
        dtr = sb("dtr", [P, T])
        banks, lo4, hi4 = S.banks, S.psum[:, 0:T], S.psum[:, T:2 * T]
        w_load = sem("w_load")
        pad_ready, xm_ready, dve_c, act_c, pool_c = sem("pad"), sem("xm_r"), sem("dve_chain"), sem("act_chain"), sem("pool_chain")
        u_psum, u_out, z_psum, z_out = sem("u_psum"), sem("u_out"), sem("z_psum"), sem("z_out")
        conv_ready, u_ready = sem("conv"), sem("u_ready")
        xd_psum, hi_ready, dtr_ready, split_done = sem("xd_psum"), sem("hi"), sem("dtr_r"), sem("split")
        dt_psum, relu_ready, soft_ready, aexp_ready = sem("dt_psum"), sem("relu"), sem("soft"), sem("aexp")
        exp_ready = sem("exp_ready")
        block = ctx.enter_context(nc.Block())

        def V(n):
            return S.vec[:, VCOL[n]:VCOL[n] + 1]

        @block.sync
        def _(sp):
            sp.dma_start(w_in_sb[:, :], dr["w_in"][d]).then_inc(w_load, 16)
            sp.dma_start(w_x[:, :, :], dr["w_x"][d].rearrange("(b p) e -> p b e", p=P)).then_inc(w_load, 16)
            sp.dma_start(w_dt[BC3:BC3 + DR, :], dr["w_dt"][d]).then_inc(w_load, 16)
            sp.wait_ge(w_load, 48)

        @block.gpsimd
        def _(pool):
            pool.memset(up[:, :, 0:KC - 1], 0.0).then_inc(pad_ready, 1)
            if d == 0:
                pool.memset(S.sel[:, :], 0.0).then_inc(pool_c, 1)
                sel = S.sel[:, :].rearrange("k (j m) -> k j m", m=P)
                for r in range(3):
                    pool.wait_ge(pool_c, r + 1)
                    pool.affine_select(out=sel, in_=sel, compare_op=ALU.not_equal, fill=1.0, base=-BC * r,
                                       pattern=[[-1, BC], [0, P]], channel_multiplier=1).then_inc(pool_c, 1)

        @block.scalar
        def _(act):
            for b in range(NB):
                act.wait_ge(u_psum, b + 1)
                act.activation(up[:, b, KC - 1:KC - 1 + T], (lo4, hi4)[b], ACT.Copy).then_inc(u_out, 1)
            for b in range(NB):
                act.wait_ge(z_psum, b + 1)
                act.activation(S.zs[:, b, :], (lo4, hi4)[b], ACT.Silu).then_inc(z_out, 1)
            for b in range(NB):
                act.wait_ge(conv_ready, b + 1)
                act.activation(S.u[:, b, :], S.dt[:, b, :], ACT.Silu).then_inc(u_ready, 1)
            act.wait_ge(xd_psum, 1)
            act.activation(dtr[BC3:BC3 + DR, :], S.psum[BC3:BC3 + DR, 0:T], ACT.Copy).then_inc(dtr_ready, 1)
            act.wait_ge(dtr_ready, 1)
            act.activation(S.bc[:, :], S.psum[0:BC3, 0:T], ACT.Copy).then_inc(hi_ready, 1)
            a0 = VCOL[f"{name}_Alog0_0"]
            act.activation(S.aneg[:, :], S.vec[:, a0:a0 + NB * NS], ACT.Exp).then_inc(aexp_ready, 1)
            for b in range(NB):
                act.wait_ge(dt_psum, b + 1)
                sf = soft[:, b, 0:T]
                act.activation(sf, (hi4, lo4)[b], ACT.Abs, bias=V(f"{name}_bdt{b}")).then_inc(act_c, 1)
            for b in range(NB):
                sf = soft[:, b, 0:T]
                act.wait_ge(act_c, b + 1)
                act.activation(sf, sf, ACT.Exp, scale=-1.0).then_inc(exp_ready, 1)
            for b in range(NB):
                sf = soft[:, b, 0:T]
                act.wait_ge(exp_ready, b + 1)
                act.activation(sf, sf, ACT.Ln, bias=1.0).then_inc(soft_ready, 1)

        @block.vector
        def _(dve):
            count = [0]

            def link(ins):
                count[0] += 1
                ins.then_inc(dve_c, 1)
                dve.wait_ge(dve_c, count[0])

            dve.tensor_scalar(xm[:, :], S.xh[:, d, :], V("norm_g"), V("norm_b"), ALU.mult, ALU.add).then_inc(xm_ready, 1)
            for b in range(NB):
                link(dve.tensor_scalar(S.diag[:, b, :], S.ident[:, :], V(f"{name}_D{b}"), None, ALU.mult))
            dve.wait_ge(pad_ready, 1)
            for b in range(NB):
                dve.wait_ge(u_out, b + 1)
                acc = S.dt[:, b, :]
                link(dve.tensor_scalar(acc, up[:, b, 0:T], V(f"{name}_convw{b}0"), V(f"{name}_convb{b}"),
                                       ALU.mult, ALU.add))
                for k in range(1, KC):
                    ins = dve.scalar_tensor_tensor(out=acc, in0=up[:, b, k:k + T], scalar=V(f"{name}_convw{b}{k}"),
                                                   in1=acc, op0=ALU.mult, op1=ALU.add)
                    if k < KC - 1:
                        link(ins)
                    else:
                        ins.then_inc(conv_ready, 1)
            dve.wait_ge(hi_ready, 1)
            link(dve.tensor_tensor(rem[0:BC3, :], S.psum[0:BC3, 0:T], S.bc[:, :], ALU.subtract))
            dve.tensor_copy(S.bc[BC:2 * BC, :], rem[BC:2 * BC, :])
            link(dve.tensor_copy(mid[2 * BC:BC3, :], rem[2 * BC:BC3, :]))
            dve.tensor_tensor(S.bc[2 * BC:BC3, :], rem[2 * BC:BC3, :], mid[2 * BC:BC3, :],
                              ALU.subtract).then_inc(split_done, 1)
            dve.wait_ge(aexp_ready, 1)
            link(dve.tensor_scalar(S.aneg[:, :], S.aneg[:, :], -1.0, None, ALU.mult))
            for b in range(NB):
                dve.wait_ge(act_c, b + 1)
                dve.tensor_scalar(S.dt[:, b, :], (hi4, lo4)[b], V(f"{name}_bdt{b}"), 0.0, ALU.add,
                                  ALU.max).then_inc(relu_ready, 1)
            for b in range(NB):
                dve.wait_ge(relu_ready, b + 1)
                dve.wait_ge(soft_ready, b + 1)
                link(dve.tensor_tensor(S.dt[:, b, :], S.dt[:, b, :], soft[:, b, 0:T], ALU.add))
                link(dve.tensor_tensor(S.dtu[:, b, :], S.dt[:, b, :], S.u[:, b, :], ALU.mult))

        @block.tensor
        def _(pe):
            pe.wait_ge(w_load, 48)
            pe.wait_ge(xm_ready, 1)
            for which, done, free in ((0, u_psum, None), (1, z_psum, u_out)):
                for b in range(NB):
                    if free is not None:
                        pe.wait_ge(free, b + 1)
                    for c in range(NCH):
                        col = DI * which + P * b
                        mm = pe.matmul(banks[4 * b + c], w_in_sb[:, col:col + P], xm[:, c * CH:(c + 1) * CH],
                                       start=True, stop=True)
                    mm.then_inc(done, 1)
            pe.wait_ge(z_out, 1)
            pe.wait_ge(u_ready, NB)
            for c in range(NCH):
                for b in range(NB):
                    mm = pe.matmul(banks[c][0:BC3 + DR, :], w_x[:, b, :], S.u[:, b, c * CH:(c + 1) * CH],
                                   start=(b == 0), stop=(b == NB - 1))
            mm.then_inc(xd_psum, 1)
            pe.wait_ge(dtr_ready, 1)
            pe.wait_ge(z_out, NB)
            for b in range(NB):
                if b:
                    pe.wait_ge(split_done, 1)
                for c in range(NCH):
                    mm = pe.matmul(banks[(4, 0)[b] + c], w_dt[BC3:BC3 + DR, P * b:P * (b + 1)],
                                   dtr[BC3:BC3 + DR, c * CH:(c + 1) * CH], start=True, stop=True)
                mm.then_inc(dt_psum, 1)


def mamba_scan_stage(nc, S, dr, d):
    name = "fb"[d]
    with ExitStack() as ctx:
        def sb(n, shape, dt=F32):
            return ctx.enter_context(nc.sbuf_tensor(f"ms{name}_{n}", shape, dt))

        def sem(n):
            return S.enter_sem(nc, f"ms{name}_{n}")

        decay = sb("decay", [P, 2, NB, CH])
        inject = sb("inject", [P, 2, NB, CH])
        crow = sb("crow", [P, 2, CH])
        hc = sb("hc", [P, 2, NB, CH])
        b_bank, c_bank, y_bank = S.banks[0:2], S.banks[2:4], S.banks[4:6]
        b_spread, b_free, c_spread, c_copied = sem("b_spread"), sem("b_free"), sem("c_spread"), sem("c_copied")
        decay_ready, scanned, weighted, summed = sem("decay_r"), sem("scanned"), sem("weighted"), sem("summed")
        y_free, first_ready, turns = sem("y_free"), sem("first_ready"), sem("turns")
        WC = NB * NS + 2 * NB
        block = ctx.enter_context(nc.Block())

        @block.scalar
        def _(act):
            act.sem_inc(c_copied, 2)
            with act.Fori(0, NCH) as c:
                for n in range(NS):
                    act.wait_ge(scanned, c * (NB * NS) + NB * (n + 1))
                    act.sem_inc(turns, 1)
                    for b in range(NB):
                        act.activation(decay[:, n % 2, b, :], S.dt[:, b, bass.ds(c * CH, CH)], ACT.Exp,
                                       scale=S.aneg[:, NS * b + n:NS * b + n + 1]).then_inc(decay_ready, 1)
                    act.wait_ge(c_spread, c * NS + (n + 1))
                    act.wait_ge(weighted, c * (NB * NS) + (NB * (n - 1) + WC))
                    act.activation(crow[:, n % 2, :], c_bank[n % 2], ACT.Copy).then_inc(c_copied, 1)

        @block.vector
        def _(dve):
            dve.sem_inc(scanned, 2 * NB)
            dve.sem_inc(b_free, 2 * NB)
            dve.sem_inc(y_free, NB)
            dve.wait_ge(first_ready, 1)
            with dve.Fori(0, NCH) as c:
                for n in range(NS):
                    dve.wait_ge(b_spread, c * NS + (n + 1))
                    dve.wait_ge(scanned, c * (NB * NS) + NB * (n + 1))
                    for b in range(NB):
                        dve.tensor_tensor(inject[:, n % 2, b, :], S.dtu[:, b, bass.ds(c * CH, CH)], b_bank[n % 2],
                                          ALU.mult).then_inc(b_free, 1)
                    for b in range(NB):
                        step = NB * n + b
                        dve.wait_ge(decay_ready, c * (NB * NS) + (step + 1))
                        dve.wait_ge(b_free, c * (NB * NS) + (step + 1 + 2 * NB))
                        dve.wait_ge(weighted, c * (NB * NS) + (step + 1 + 2 * NB))
                        dve.tensor_tensor_scan(S.h[:, b, n, :], decay[:, n % 2, b, :], inject[:, n % 2, b, :],
                                               S.h[:, b, n, CH - 1:CH], ALU.mult, ALU.add).then_inc(scanned, 1)
                dve.wait_ge(summed, c * NS + (NS + 2))
                for b in range(NB):
                    gated = S.zs[:, b, bass.ds(c * CH, CH)]
                    dve.tensor_tensor(gated, gated, y_bank[b], ALU.mult).then_inc(y_free, 1)

        @block.gpsimd
        def _(pool):
            pool.sem_inc(weighted, WC)
            pool.memset(S.h[:, :, :, CH - 1:CH], 0.0).then_inc(first_ready, 1)
            with pool.Fori(0, NCH) as c:
                for n in range(NS):
                    pool.wait_ge(c_copied, c * NS + (n + 3))
                    pool.wait_ge(summed, c * NS + (n + 1))
                    for b in range(NB):
                        pool.wait_ge(scanned, c * (NB * NS) + (NB * n + b + 1 + 2 * NB))
                        pool.tensor_tensor(hc[:, n % 2, b, :], S.h[:, b, n, :], crow[:, n % 2, :],
                                           ALU.mult).then_inc(weighted, 1)

        @block.tensor
        def _(pe):
            pe.sem_inc(summed, 2)

            def spread(c, n):
                cols = bass.ds(c * CH, CH)
                pe.wait_ge(b_free, c * (NB * NS) + NB * (n + 1))
                pe.matmul(b_bank[n % 2], S.sel[:, P * n:P * (n + 1)], S.bc[:, cols],
                          start=True, stop=True).then_inc(b_spread, 1)
                pe.wait_ge(c_copied, c * NS + (n + 1))
                pe.matmul(c_bank[n % 2], S.sel[:, P * (NS + n):P * (NS + n + 1)], S.bc[:, cols],
                          start=True, stop=True).then_inc(c_spread, 1)

            with pe.Fori(0, NCH) as c:
                spread(c, 0)
                spread(c, 1)
                for b in range(NB):
                    pe.wait_ge(y_free, c * NB + (b + 1))
                    pe.matmul(y_bank[b], S.diag[:, b, :], S.u[:, b, bass.ds(c * CH, CH)],
                              start=True, stop=False)
                for n in range(NS):
                    for b in range(NB):
                        pe.wait_ge(weighted, c * (NB * NS) + (NB * n + b + 1 + WC))
                        mm = pe.matmul(y_bank[b], S.ident[:, :], hc[:, n % 2, b, :],
                                       start=False, stop=(n == NS - 1))
                    mm.then_inc(summed, 1)
                    if n + 2 < NS:
                        spread(c, n + 2)


def mamba_out_stage(nc, S, dr, d):
    name = "fb"[d]
    with ExitStack() as ctx:
        def sem(n):
            return S.enter_sem(nc, f"mo{name}_{n}")

        w_out = ctx.enter_context(nc.sbuf_tensor(f"mo{name}_w", [P, NB, P], F32))
        nat = ctx.enter_context(nc.sbuf_tensor(f"mo{name}_nat", [P, NCH, CH], F32))
        w_load, out_psum, nat_ready, turned, added = sem("w_load"), sem("psum"), sem("nat_ready"), sem("turned"), sem("added")
        banks = S.banks
        block = ctx.enter_context(nc.Block())

        @block.sync
        def _(sp):
            sp.dma_start(w_out[:, :, :], dr["w_out"][d].rearrange("(b p) e -> p b e", p=P)).then_inc(w_load, 16)
            sp.wait_ge(w_load, 16)

        @block.tensor
        def _(pe):
            pe.wait_ge(w_load, 16)
            for c in range(NCH):
                for i in range(TPC):
                    t = TPC * c + i
                    for b in range(NB):
                        mm = pe.matmul(banks[c][:, P * i:P * (i + 1)], S.zs[:, b, P * t:P * (t + 1)], w_out[:, b, :],
                                       start=(b == 0), stop=(b == NB - 1))
                mm.then_inc(out_psum, 1)
            if d:
                for c in range(NCH):
                    pe.wait_ge(nat_ready, c + 1)
                    pe.matmul(banks[4 + c], S.flip[:, :], nat[:, c, :], start=True, stop=True).then_inc(turned, 1)

        @block.scalar
        def _(act):
            if d:
                for c in range(NCH):
                    act.wait_ge(out_psum, c + 1)
                    act.activation(nat[:, c, :], banks[c], ACT.Copy).then_inc(nat_ready, 1)

        @block.vector
        def _(dve):
            for c in range(NCH):
                if d == 0:
                    dve.wait_ge(out_psum, c + 1)
                    r = S.res[:, TPC * c:TPC * (c + 1), :]
                    dve.tensor_tensor(r, r, banks[c].rearrange("p (i d) -> p i d", d=P), ALU.add).then_inc(added, 1)
                else:
                    dve.wait_ge(turned, c + 1)
                    for i in range(TPC):
                        r = S.res[:, NT - 1 - (TPC * c + i), :]
                        dve.tensor_tensor(r, r, banks[4 + c][:, P * i:P * (i + 1)], ALU.add).then_inc(added, 1)


def mamba(nc, S, dr):
    with ExitStack() as ctx:
        def sb(n, shape, dt=F32):
            return ctx.enter_context(nc.sbuf_tensor(f"m_{n}", shape, dt))

        S.u, S.zs, S.dt, S.dtu = (sb(n, [P, NB, T]) for n in ("u", "zs", "dt", "dtu"))
        S.bc = sb("bc", [BC3, T], BF16)
        S.sel = sb("sel", [BC3, BC * P], BF16)
        S.aneg = sb("aneg", [P, NB * NS])
        S.diag = sb("diag", [P, NB, P])
        for d in range(2):
            mamba_prep_stage(nc, S, dr, d)
            S.end_stage(nc)
            with ExitStack() as c2:
                S.h = c2.enter_context(nc.sbuf_tensor(f"m_h{d}", [P, NB, NS, CH], F32))
                mamba_scan_stage(nc, S, dr, d)
                S.end_stage(nc)
            mamba_out_stage(nc, S, dr, d)
            S.end_stage(nc)


def moe_prep_stage(nc, S, dr):
    with ExitStack() as ctx:
        def sb(n, shape, dt=F32):
            return ctx.enter_context(nc.sbuf_tensor(f"xp_{n}", shape, dt))

        def sem(n):
            return S.enter_sem(nc, f"xp_{n}")

        st6, mv = sb("st6", [P, NT, 6]), sb("mv", [P, NT, 2])
        lnv, rstd = sb("lnv", [P, NT]), sb("rstd", [P, NT])
        xn = sb("xn", [P, NT, P])
        gw, gb, b2 = sb("gw", [P, NE]), sb("gb", [P, NE]), sb("b2", [NE, P])
        rank_i, rank = sb("rank_i", [P, NE], I32), sb("rank", [P, NE])
        lg, top, pick = sb("lg", [P, NT, NE]), sb("top", [P, NT]), sb("pick", [P, NT, NE])
        ohT = sb("ohT", [NE, T])
        banks = S.banks
        w_load, rank_ready, dve_c, act_c = sem("w_load"), sem("rank"), sem("dve_chain"), sem("act_chain")
        var_ready, rstd_ready, xn_ready, xn_psum, hn_ready = sem("var"), sem("rstd"), sem("xn_r"), sem("xn_psum"), sem("hn_r")
        lg_psum, oh_ready, ohT_psum, ohT_ready, b2_psum = sem("lg_psum"), sem("oh_r"), sem("ohT_psum"), sem("ohT_r"), sem("b2_psum")
        block = ctx.enter_context(nc.Block())

        def V(n):
            return S.vec[:, VCOL[n]:VCOL[n] + 1]

        @block.sync
        def _(sp):
            sp.dma_start(gw[:, :], dr["gate_w"]).then_inc(w_load, 16)
            sp.dma_start(gb[:, :], dr["gate_b"]).then_inc(w_load, 16)
            sp.dma_start(b2[:, :], dr["b2"]).then_inc(w_load, 16)
            sp.wait_ge(w_load, 48)

        @block.gpsimd
        def _(pool):
            pool.iota(rank_i[:, :], pattern=[[-1, NE]], base=NE, channel_multiplier=0).then_inc(rank_ready, 1)

        @block.scalar
        def _(act):
            act.wait_ge(var_ready, 1)
            act.activation(lnv[:, :], lnv[:, :], ACT.Ln).then_inc(act_c, 1)
            act.wait_ge(act_c, 1)
            act.activation(rstd[:, :], lnv[:, :], ACT.Exp, scale=-0.5).then_inc(rstd_ready, 1)
            for c in range(NCH):
                act.wait_ge(xn_psum, c + 1)
                act.activation(S.hn2[:, c * CH:(c + 1) * CH], banks[c], ACT.Identity, bias=V("ln2_b"),
                               scale=V("ln2_g")).then_inc(hn_ready, 1)
            for c in range(NCH):
                act.wait_ge(ohT_psum, c + 1)
                act.activation(ohT[:, c * CH:(c + 1) * CH], banks[c][0:NE, :], ACT.Copy).then_inc(ohT_ready, 1)

        @block.vector
        def _(dve):
            count = [0]

            def link(ins):
                count[0] += 1
                ins.then_inc(dve_c, 1)
                dve.wait_ge(dve_c, count[0])

            for i in range(NT):
                last = dve.bn_stats(st6[:, i, :], S.xn1[:, i, :])
            link(last)
            for i in range(NT):
                last = dve.bn_aggr(mv[:, i, :], st6[:, i, :])
            link(last)
            dve.tensor_scalar(lnv[:, :], mv[:, :, 1], EPS, None, ALU.add).then_inc(var_ready, 1)
            dve.wait_ge(rstd_ready, 1)
            for i in range(NT):
                dve.tensor_scalar(xn[:, i, :], S.xn1[:, i, :], mv[:, i, 0:1], rstd[:, i:i + 1],
                                  ALU.subtract, ALU.mult).then_inc(xn_ready, 1)
            dve.wait_ge(rank_ready, 1)
            link(dve.tensor_copy(rank[:, :], rank_i[:, :]))
            dve.wait_ge(w_load, 48)
            dve.wait_ge(lg_psum, 1)
            link(dve.tensor_tensor(lg[:, :, :], banks[4][:, 0:NT * NE].rearrange("p (i e) -> p i e", e=NE),
                                   gb[:, :].unsqueeze(1).to_broadcast([P, NT, NE]), ALU.add))
            link(dve.tensor_reduce(top[:, :], lg[:, :, :], AX.X, ALU.max))
            link(dve.tensor_tensor(pick[:, :, :], lg[:, :, :], top[:, :].unsqueeze(2).to_broadcast([P, NT, NE]),
                                   ALU.is_ge))
            link(dve.tensor_tensor(pick[:, :, :], pick[:, :, :], rank[:, :].unsqueeze(1).to_broadcast([P, NT, NE]),
                                   ALU.mult))
            link(dve.tensor_reduce(top[:, :], pick[:, :, :], AX.X, ALU.max))
            dve.tensor_tensor(S.oh[:, :, :], pick[:, :, :], top[:, :].unsqueeze(2).to_broadcast([P, NT, NE]),
                              ALU.is_equal).then_inc(oh_ready, 1)
            for c in range(NCH):
                dve.wait_ge(b2_psum, c + 1)
                r = S.res[:, TPC * c:TPC * (c + 1), :]
                dve.tensor_tensor(r, r, banks[4 + c].rearrange("p (i d) -> p i d", d=P), ALU.add).then_inc(dve_c, 1)

        @block.tensor
        def _(pe):
            for c in range(NCH):
                pe.wait_ge(xn_ready, TPC * (c + 1))
                for i in range(TPC):
                    mm = pe.transpose(banks[c][:, P * i:P * (i + 1)], xn[:, TPC * c + i, :], S.ident[:, :])
                mm.then_inc(xn_psum, 1)
            pe.wait_ge(w_load, 48)
            pe.wait_ge(hn_ready, NCH)
            for t in range(NT):
                mm = pe.matmul(banks[4][:, NE * t:NE * (t + 1)], S.hn2[:, P * t:P * (t + 1)], gw[:, :],
                               start=True, stop=True)
            mm.then_inc(lg_psum, 1)
            pe.wait_ge(oh_ready, 1)
            for c in range(NCH):
                for i in range(TPC):
                    mm = pe.transpose(banks[c][0:NE, P * i:P * (i + 1)], S.oh[:, TPC * c + i, :], S.ident[:, :])
                mm.then_inc(ohT_psum, 1)
            for c in range(NCH):
                pe.wait_ge(ohT_ready, c + 1)
                for i in range(TPC):
                    t = TPC * c + i
                    mm = pe.matmul(banks[4 + c][:, P * i:P * (i + 1)], ohT[:, P * t:P * (t + 1)], b2[:, :],
                                   start=True, stop=True)
                mm.then_inc(b2_psum, 1)


def moe_stage(nc, S, dr):
    with ExitStack() as ctx:
        def sb(n, shape, dt=F32):
            return ctx.enter_context(nc.sbuf_tensor(f"xe_{n}", shape, dt))

        def sem(n):
            return S.enter_sem(nc, f"xe_{n}")

        w1, w2, b1 = sb("w1", [P, 2, NF]), sb("w2", [P, 2, NFB, P]), sb("b1", [P, 2, NFB])
        mid = sb("mid", [P, 2, NFB, CH])
        banks = S.banks
        w_load = [sem("w_load0"), sem("w_load1")]
        mid_psum, mid_ready, y_psum, added = sem("mid_psum"), sem("mid_ready"), sem("y_psum"), sem("added")
        block = ctx.enter_context(nc.Block())
        NP = NE // 2

        @block.sync
        def _(sp):
            def load(e, par):
                sp.dma_start(w1[:, par, :], dr["w1"][bass.ds(e, 1)].rearrange("o h f -> h (o f)")).then_inc(w_load[par], 16)
                sp.dma_start(w2[:, par, :, :], dr["w2"][bass.ds(e, 1)].rearrange("o (b p) h -> p (o b) h", p=P))\
                    .then_inc(w_load[par], 16)
                sp.dma_start(b1[:, par, :], dr["b1"][bass.ds(e, 1)].rearrange("o p b -> p (o b)")).then_inc(w_load[par], 16)

            load(0, 0)
            load(1, 1)
            with sp.Fori(0, NP - 1) as ep:
                for par in range(2):
                    sp.wait_ge(y_psum, ep * (2 * NCH) + (NCH * (par + 1) + 2))
                    load(ep * 2 + (2 + par), par)

        @block.scalar
        def _(act):
            with act.Fori(0, NP) as ep:
                for par in range(2):
                    for c in range(NCH):
                        step = NCH * par + c
                        act.wait_ge(y_psum, ep * (2 * NCH) + (step + 1))
                        for f in range(NFB):
                            act.wait_ge(mid_psum, ep * (2 * NCH * NFB) + (NFB * step + f + 1))
                            act.activation(mid[:, c % 2, f, :], banks[f], ACT.Relu,
                                           bias=b1[:, par, f:f + 1]).then_inc(mid_ready, 1)

        @block.vector
        def _(dve):
            dve.sem_inc(added, 2)
            with dve.Fori(0, NP) as ep:
                for par in range(2):
                    for c in range(NCH):
                        step = NCH * par + c
                        dve.wait_ge(y_psum, ep * (2 * NCH) + (step + 3))
                        for i in range(TPC):
                            t = TPC * c + i
                            ins = dve.scalar_tensor_tensor(
                                out=S.res[:, t, :], in0=banks[4 + c % 2][:, P * i:P * (i + 1)],
                                scalar=S.oh[:, t, bass.ds(ep * 2 + par, 1)], in1=S.res[:, t, :],
                                op0=ALU.mult, op1=ALU.add)
                        ins.then_inc(added, 1)
                        dve.wait_ge(added, ep * (2 * NCH) + (step + 3))

        @block.tensor
        def _(pe):
            pe.sem_inc(mid_ready, NFB)
            pe.sem_inc(y_psum, 2)

            def hidden(ep, par, c):
                step = NCH * par + c
                for f in range(NFB):
                    pe.wait_ge(mid_ready, ep * (2 * NCH * NFB) + (NFB * step + f + 1))
                    pe.matmul(banks[f], w1[:, par, P * f:P * (f + 1)], S.hn2[:, c * CH:(c + 1) * CH],
                              start=True, stop=True).then_inc(mid_psum, 1)

            def output(ep, par, c):
                step = NCH * par + c
                pe.wait_ge(added, ep * (2 * NCH) + (step + 1))
                pe.wait_ge(mid_ready, ep * (2 * NCH * NFB) + (NFB * (step + 2)))
                for i in range(TPC):
                    for f in range(NFB):
                        mm = pe.matmul(banks[4 + c % 2][:, P * i:P * (i + 1)], mid[:, c % 2, f, P * i:P * (i + 1)],
                                       w2[:, par, f, :], start=(f == 0), stop=(f == NFB - 1))
                mm.then_inc(y_psum, 1)

            with pe.Fori(0, NP) as ep:
                for par in range(2):
                    for c in range(NCH):
                        if c == 0:
                            pe.wait_ge(w_load[par], ep * 48 + 48)
                        hidden(ep, par, c)
                        if par or c:
                            output(ep, *divmod(NCH * par + c - 1, NCH))
                output(ep, 1, NCH - 1)


def moe(nc, S, dr):
    with ExitStack() as ctx:
        S.hn2 = ctx.enter_context(nc.sbuf_tensor("x_hn2", [P, T], F32))
        S.oh = ctx.enter_context(nc.sbuf_tensor("x_oh", [P, NT, NE], F32))
        moe_prep_stage(nc, S, dr)
        S.end_stage(nc)
        moe_stage(nc, S, dr)
        S.end_stage(nc)



def build(nc, dr, out, upto=9):
    with ExitStack() as ctx:
        S = Shared()
        S.sems = []
        S.ident = ctx.enter_context(nc.sbuf_tensor("ident", [P, P], F32))
        S.flip = ctx.enter_context(nc.sbuf_tensor("flip", [P, P], F32))
        S.vec = ctx.enter_context(nc.sbuf_tensor("vec", [P, NV], F32))
        S.res = ctx.enter_context(nc.sbuf_tensor("res", [P, NT, P], F32))
        S.xn1 = ctx.enter_context(nc.sbuf_tensor("xn1", [P, NT, P], F32))
        S.xh = ctx.enter_context(nc.sbuf_tensor("xh", [P, 2, T], F32))
        psum = ctx.enter_context(nc.psum_tensor("psum", [P, 8 * CH], F32))
        S.psum = psum
        S.banks = [psum[:, i * CH:(i + 1) * CH] for i in range(8)]
        S.sc01, S.sc23 = psum[:, 0:2 * CH], psum[:, 2 * CH:4 * CH]
        layer0_stage(nc, S, dr)
        S.end_stage(nc)
        for st in STAGES[:upto]:
            st(nc, S, dr)
        with nc.semaphore("out_done") as out_done, nc.Block() as block:
            @block.sync
            def _(sp):
                sp.dma_start(natural(out), S.res[:, :, :]).then_inc(out_done, 16)
                sp.wait_ge(out_done, 16)


STAGES = [attention, mamba, moe]


def pack(inputs):
    a = {k: np.asarray(v) for k, v in inputs.items()}
    out = {"x": a["L0_attn_x"]}
    col = {"init_re": a["L0_attn_phazor_init_re"], "init_im": a["L0_attn_phazor_init_im"],
           "angle": a["L0_attn_phazor_angle"], "lnml": a["L0_attn_ln_minus_ln_phazor_abs"],
           "lc_re": a["L0_attn_last_conv_re"], "lc_im": a["L0_attn_last_conv_im"],
           "ln_scale": a["L0_attn_ln_phazor_scale"], "mu_r": a["L0_ffn_mu_r"], "mu_k": a["L0_ffn_mu_k"],
           "norm_g": a["L1_attn_norm_g"], "norm_b": a["L1_attn_norm_b"], "bq": a["L1_ffn_bq"], "bk": a["L1_ffn_bk"]}
    for n in ("ln1_g", "ln1_b", "ln2_g", "ln2_b"):
        col[n] = a[f"L1_ffn_{n}"]
    for d in "fb":
        for b in range(NB):
            rows = slice(P * b, P * (b + 1))
            for n in ("convb", "bdt", "D"):
                col[f"{d}_{n}{b}"] = a[f"L1_attn_{d}_{n}"][rows]
            for k in range(KC):
                col[f"{d}_convw{b}{k}"] = a[f"L1_attn_{d}_convw"][rows, 0, k]
            for s in range(NS):
                col[f"{d}_Alog{b}_{s}"] = a[f"L1_attn_{d}_Alog"][rows, s]
    out["b1"] = a["L1_ffn_b1"].reshape(NE, NFB, P).transpose(0, 2, 1)
    out["vecs"] = np.stack([col[n] for n in VECS], axis=1)
    out["w_mix"] = np.stack([a[f"L0_ffn_W_{n}"].T for n in "rkv"])
    for n in ("wq", "wk", "wv", "wo", "gate_w"):
        out[n] = a[f"L1_ffn_{n}"]
    for n in ("bv", "bo", "gate_b"):
        out[n] = np.broadcast_to(a[f"L1_ffn_{n}"][None, :], (P,) + a[f"L1_ffn_{n}"].shape)
    out["w1"], out["w2"], out["b2"] = a["L1_ffn_w1"], a["L1_ffn_w2"], a["L1_ffn_b2"]
    w_in, w_x, w_dt, w_out = [], [], [], []
    for d in "fb":
        w_in.append(a[f"L1_attn_{d}_Win"].T)
        wx = a[f"L1_attn_{d}_Wx"].T
        bc = wx[:, DR:]
        w_x.append(np.concatenate([bc, bc, bc, wx[:, :DR]], axis=1))
        w_dt.append(a[f"L1_attn_{d}_Wdt"].T)
        w_out.append(a[f"L1_attn_{d}_Wout"].T)
    out["w_in"], out["w_x"], out["w_dt"], out["w_out"] = (np.stack(w) for w in (w_in, w_x, w_dt, w_out))
    return {k: np.ascontiguousarray(v) for k, v in out.items()}


def kernel(**inputs):
    import concourse.bacc as bacc
    from concourse.bass_utils import run_bass_kernel_spmd

    nc = bacc.Bacc("TRN2", target_bir_lowering=False, num_devices=1)
    arrays = pack(inputs)
    dr = {k: nc.dram_tensor(f"in_{k}", v.shape, mybir.dt.from_np(v.dtype), kind="ExternalInput").ap()
          for k, v in arrays.items()}
    out = nc.dram_tensor("out_0", (1, T, P), F32, kind="ExternalOutput").ap()
    build(nc, dr, out)
    r = run_bass_kernel_spmd(nc, [{f"in_{k}": v for k, v in arrays.items()}], core_ids=[0])
    return r.results[0]["out_0"]
```
